# Optimizing a Trainium2 kernel written in Bass

```python
import numpy as np
import jax
import jax.numpy as jnp

def _softmax(x, axis=-1):
    return jax.nn.softmax(x, axis=axis)

def _gelu(x):
    return jax.nn.gelu(x, approximate=True)

def _silu(x):
    return jax.nn.silu(x)

def _sigmoid(x):
    return jax.nn.sigmoid(x)

def _layernorm(x, axis=-1, eps=1e-05):
    m = jnp.mean(x, axis=axis, keepdims=True)
    v = jnp.var(x, axis=axis, keepdims=True)
    return (x - m) / jnp.sqrt(v + eps)

def _scatter_add(tgt, idx, src, axis=0):
    return tgt.at[idx].add(src)

def _segment_sum(src, seg, n):
    return jax.ops.segment_sum(src, seg, n)
kernel_name = 'mk_gnn_preln_d4_gnn_r32_8f97af'

def setup_inputs(seed: int=0):
    np.random.seed(seed)
    _w = jnp.asarray

    def _rec_inputs():
        import jax
        import jax.numpy as jnp
        _gk = jax.random.key(seed)
        x = -0.0008691 + 1 * jax.random.normal(jax.random.fold_in(_gk, 1), (3125, 128), jnp.float32)
        _s = jax.random.randint(jax.random.fold_in(_gk, 2), (50000,), 0, 3125, jnp.int32)
        _d = jax.random.randint(jax.random.fold_in(_gk, 3), (50000,), 0, 3125, jnp.int32)
        _loop = jnp.arange(3125, dtype=jnp.int32)
        src = jnp.concatenate([_s, _d, _loop])
        dst = jnp.concatenate([_d, _s, _loop])
        _o = jnp.argsort(dst, stable=True)
        src = src[_o]
        dst = dst[_o]
        edge_attr_32 = 0.000196303 + 1.00016 * jax.random.normal(jax.random.fold_in(_gk, 11), (103125, 32), jnp.float32)
        return (x, src, dst, edge_attr_32)
    x, src, dst, edge_attr_32 = _rec_inputs()

    def _L0_gnn_setup():
        import jax, jax.numpy as jnp
        import numpy as np
        N_NODES = 10000
        key = jax.random.key(seed)
        k1, k2, k3 = jax.random.split(key, 3)
        N, E, D, D_OUT = (N_NODES, 20000, 128, 128)
        x = jax.random.normal(k1, (N, D), dtype=jnp.float32)
        edge_index = jax.random.randint(k2, (2, E), 0, N, dtype=jnp.int64)
        limit = float(np.sqrt(6.0 / (2 * D + D_OUT)))
        W_out = jax.random.uniform(k3, (D_OUT, 2 * D), dtype=jnp.float32, minval=-limit, maxval=limit)
        b_out = jnp.zeros((D_OUT,), dtype=jnp.float32)
        return {'x': x, 'edge_index': edge_index, 'W_out': W_out, 'b_out': b_out}
    _L0_gnn_all = _L0_gnn_setup()
    _L0_gnn_in = {k: v for k, v in _L0_gnn_all.items() if k in ('W_out', 'b_out')}
    del _L0_gnn_all

    def _L1_gnn_setup():
        import jax, jax.numpy as jnp
        import numpy as np
        N_NODES = 50000
        key = jax.random.key(seed)
        k1, k2, k3 = jax.random.split(key, 3)
        H = jax.random.normal(k1, (N_NODES, 128), dtype=jnp.float32)
        edge_index = jax.random.randint(k2, (2, 25000), 0, N_NODES, dtype=jnp.int64)
        W = jax.random.normal(k3, (128, 128), dtype=jnp.float32) * jnp.sqrt(2.0 / 128.0)
        return {'H': H, 'edge_index': edge_index, 'W': W}
    _L1_gnn_all = _L1_gnn_setup()
    _L1_gnn_in = {k: v for k, v in _L1_gnn_all.items() if k in ('W',)}
    del _L1_gnn_all

    def _L2_gnn_setup():
        import jax, jax.numpy as jnp
        import numpy as np
        N, E = (50000, 25000)
        D_IN, HID, H, C, E_DIM = (128, 128, 4, 32, 32)
        key = jax.random.key(seed)
        ks = jax.random.split(key, 16)

        def lin(k, fan_in, fan_out):
            return jax.random.normal(k, (fan_in, fan_out), jnp.float32) / np.sqrt(fan_in)
        return {'x': jax.random.normal(ks[0], (N, D_IN), jnp.float32), 'edge_index': jax.random.randint(ks[1], (2, E), 0, N, jnp.int32), 'edge_attr': jax.random.normal(ks[2], (E, E_DIM), jnp.float32), 'Wq': lin(ks[3], D_IN, HID), 'bq': jnp.zeros((HID,), jnp.float32), 'Wk': lin(ks[4], D_IN, HID), 'bk': jnp.zeros((HID,), jnp.float32), 'Wv': lin(ks[5], D_IN, HID), 'bv': jnp.zeros((HID,), jnp.float32), 'We': lin(ks[6], E_DIM, HID), 'Wskip': lin(ks[7], D_IN, HID), 'bskip': jnp.zeros((HID,), jnp.float32), 'W1': lin(ks[8], HID, HID), 'b1': jnp.zeros((HID,), jnp.float32), 'W2': lin(ks[9], HID, HID), 'b2': jnp.zeros((HID,), jnp.float32)}
    _L2_gnn_all = _L2_gnn_setup()
    _L2_gnn_in = {k: v for k, v in _L2_gnn_all.items() if k in ('Wq', 'bq', 'Wk', 'bk', 'Wv', 'bv', 'We', 'Wskip', 'bskip', 'W1', 'b1', 'W2', 'b2')}
    del _L2_gnn_all

    def _L3_gnn_setup():
        import jax, jax.numpy as jnp
        import numpy as np
        N_NODES = 50000
        N_EDGES = 18750
        IN_DIM = 128
        OUT_DIM = 128
        EPS = 1e-05

        def _layernorm(x, gamma, beta):
            mu = jnp.mean(x, axis=-1, keepdims=True)
            var = jnp.mean(jnp.square(x - mu), axis=-1, keepdims=True)
            return (x - mu) * jax.lax.rsqrt(var + EPS) * gamma + beta
        key = jax.random.key(seed)
        k1, k2, k3 = jax.random.split(key, 3)
        h = jax.random.normal(k1, (N_NODES, IN_DIM), dtype=jnp.float32)
        edge_index = jax.random.randint(k2, (2, N_EDGES), 0, N_NODES, dtype=jnp.int64)
        ln_gamma = jnp.ones((IN_DIM,), dtype=jnp.float32)
        ln_beta = jnp.zeros((IN_DIM,), dtype=jnp.float32)
        W = jax.random.normal(k3, (OUT_DIM, 2 * IN_DIM), dtype=jnp.float32) * (1.0 / np.sqrt(2 * IN_DIM))
        b = jnp.zeros((OUT_DIM,), dtype=jnp.float32)
        return {'h': h, 'edge_index': edge_index, 'ln_gamma': ln_gamma, 'ln_beta': ln_beta, 'W': W, 'b': b}
    _L3_gnn_all = _L3_gnn_setup()
    _L3_gnn_in = {k: v for k, v in _L3_gnn_all.items() if k in ('ln_gamma', 'ln_beta', 'W', 'b')}
    del _L3_gnn_all
    return {'x': x, 'src': src, 'dst': dst, 'edge_attr_32': edge_attr_32, 'L0_gnn_W_out': _L0_gnn_in['W_out'], 'L0_gnn_b_out': _L0_gnn_in['b_out'], 'L1_gnn_W': _L1_gnn_in['W'], 'L2_gnn_Wq': _L2_gnn_in['Wq'], 'L2_gnn_bq': _L2_gnn_in['bq'], 'L2_gnn_Wk': _L2_gnn_in['Wk'], 'L2_gnn_bk': _L2_gnn_in['bk'], 'L2_gnn_Wv': _L2_gnn_in['Wv'], 'L2_gnn_bv': _L2_gnn_in['bv'], 'L2_gnn_We': _L2_gnn_in['We'], 'L2_gnn_Wskip': _L2_gnn_in['Wskip'], 'L2_gnn_bskip': _L2_gnn_in['bskip'], 'L2_gnn_W1': _L2_gnn_in['W1'], 'L2_gnn_b1': _L2_gnn_in['b1'], 'L2_gnn_W2': _L2_gnn_in['W2'], 'L2_gnn_b2': _L2_gnn_in['b2'], 'L3_gnn_ln_gamma': _L3_gnn_in['ln_gamma'], 'L3_gnn_ln_beta': _L3_gnn_in['ln_beta'], 'L3_gnn_W': _L3_gnn_in['W'], 'L3_gnn_b': _L3_gnn_in['b']}

def reference(x, src, dst, edge_attr_32, L0_gnn_W_out, L0_gnn_b_out, L1_gnn_W, L2_gnn_Wq, L2_gnn_bq, L2_gnn_Wk, L2_gnn_bk, L2_gnn_Wv, L2_gnn_bv, L2_gnn_We, L2_gnn_Wskip, L2_gnn_bskip, L2_gnn_W1, L2_gnn_b1, L2_gnn_W2, L2_gnn_b2, L3_gnn_ln_gamma, L3_gnn_ln_beta, L3_gnn_W, L3_gnn_b):
    import jax
    import jax.numpy as jnp

    def _L0_gnn_ref(x, edge_index, W_out, b_out):
        import jax, jax.numpy as jnp
        import numpy as np
        N_NODES = 10000
        row, col = (edge_index[0], edge_index[1])
        N = x.shape[0]
        neigh_sum = jax.ops.segment_sum(x[row], col, num_segments=N)
        count = jax.ops.segment_sum(jnp.ones_like(col, dtype=x.dtype), col, num_segments=N)
        out = neigh_sum / jnp.clip(count, 1.0)[:, None]
        h = jnp.concatenate([x, out], axis=-1)
        return h @ W_out.T + b_out

    def _L1_gnn_ref(H, edge_index, W):
        import jax, jax.numpy as jnp
        import numpy as np
        N_NODES = 50000
        src, dst = (edge_index[0], edge_index[1])
        new_H = jax.ops.segment_sum(H[src], dst, num_segments=H.shape[0])
        out = (H + new_H) @ W
        return jax.nn.relu(out)

    def _L2_gnn_ref(x, edge_index, edge_attr, Wq, bq, Wk, bk, Wv, bv, We, Wskip, bskip, W1, b1, W2, b2):
        import jax, jax.numpy as jnp
        import numpy as np
        N, E = (50000, 25000)
        D_IN, HID, H, C, E_DIM = (128, 128, 4, 32, 32)
        src, dst = (edge_index[0], edge_index[1])
        n = x.shape[0]
        q = (x @ Wq + bq).reshape(n, H, C)
        k = (x @ Wk + bk).reshape(n, H, C)
        v = (x @ Wv + bv).reshape(n, H, C)
        e = (edge_attr @ We).reshape(-1, H, C)
        kj = k[src] + e
        vj = v[src] + e
        alpha = jnp.einsum('ehc,ehc->eh', q[dst], kj) / np.sqrt(C)
        amax = jax.ops.segment_max(alpha, dst, num_segments=n)
        amax = jnp.where(jnp.isfinite(amax), amax, 0.0)
        ex = jnp.exp(alpha - amax[dst])
        denom = jax.ops.segment_sum(ex, dst, num_segments=n)
        alpha = ex / (denom[dst] + 1e-16)
        agg = jax.ops.segment_sum(vj * alpha[:, :, None], dst, num_segments=n)
        out = agg.reshape(n, HID) + (x @ Wskip + bskip)
        h = jax.nn.gelu(out @ W1 + b1, approximate=True)
        h = jax.nn.gelu(h @ W2 + b2, approximate=True)
        return out + h

    def _L3_gnn_ref(h, edge_index, ln_gamma, ln_beta, W, b):
        import jax, jax.numpy as jnp
        import numpy as np
        N_NODES = 50000
        N_EDGES = 18750
        IN_DIM = 128
        OUT_DIM = 128
        EPS = 1e-05

        def _layernorm(x, gamma, beta):
            mu = jnp.mean(x, axis=-1, keepdims=True)
            var = jnp.mean(jnp.square(x - mu), axis=-1, keepdims=True)
            return (x - mu) * jax.lax.rsqrt(var + EPS) * gamma + beta
        src, dst = (edge_index[0], edge_index[1])
        n = h.shape[0]
        hn = _layernorm(h, ln_gamma, ln_beta)
        ones = jnp.ones((src.shape[0],), dtype=h.dtype)
        deg_out = jnp.clip(jax.ops.segment_sum(ones, src, num_segments=n), 1.0)
        deg_in = jnp.clip(jax.ops.segment_sum(ones, dst, num_segments=n), 1.0)
        inv_sqrt_out = jax.lax.rsqrt(deg_out)
        inv_sqrt_in = jax.lax.rsqrt(deg_in)
        msg_src = hn * inv_sqrt_out[:, None]
        gathered = msg_src[src]
        agg = jax.ops.segment_sum(gathered, dst, num_segments=n)
        message = agg * inv_sqrt_in[:, None]
        cat = jnp.concatenate([hn, message], axis=1)
        return cat @ W.T + b
    edge_index = jnp.stack([src, dst])
    h = jnp.maximum(_layernorm(x, axis=-1), 0.0)
    x = x + _L0_gnn_ref(h, edge_index, L0_gnn_W_out, L0_gnn_b_out)
    h = jnp.maximum(_layernorm(x, axis=-1), 0.0)
    x = x + _L1_gnn_ref(h, edge_index, L1_gnn_W)
    h = jnp.maximum(_layernorm(x, axis=-1), 0.0)
    x = x + _L2_gnn_ref(h, edge_index, edge_attr_32, L2_gnn_Wq, L2_gnn_bq, L2_gnn_Wk, L2_gnn_bk, L2_gnn_Wv, L2_gnn_bv, L2_gnn_We, L2_gnn_Wskip, L2_gnn_bskip, L2_gnn_W1, L2_gnn_b1, L2_gnn_W2, L2_gnn_b2)
    h = jnp.maximum(_layernorm(x, axis=-1), 0.0)
    x = x + _L3_gnn_ref(h, edge_index, L3_gnn_ln_gamma, L3_gnn_ln_beta, L3_gnn_W, L3_gnn_b)
    return x

_drawn_inputs = setup_inputs


def setup_inputs(seed=0):
    import zlib

    import numpy as np

    out = dict(_drawn_inputs(seed))
    spreads = {'L0_gnn_b_out': (0.0, 0.1),
     'L2_gnn_bq': (0.0, 0.8),
     'L2_gnn_bk': (0.0, 2.0),
     'L2_gnn_bv': (0.0, 0.8),
     'L2_gnn_bskip': (0.0, 0.8),
     'L2_gnn_b1': (0.0, 2.0),
     'L2_gnn_b2': (0.0, 2.0),
     'L3_gnn_ln_gamma': (1.0, 0.6),
     'L3_gnn_ln_beta': (0.0, 0.8),
     'L3_gnn_b': (0.0, 0.8)}
    factors = {'edge_attr_32': 3.264, 'L2_gnn_Wq': 2.957, 'L2_gnn_Wk': 8.0, 'L2_gnn_We': 3.003}
    for name, (base, spread) in spreads.items():
        noise = np.random.default_rng([zlib.crc32(name.encode()), seed]).standard_normal(out[name].shape)
        drawn = base * np.exp(spread * noise) if base else spread * noise
        out[name] = jnp.asarray(drawn.astype(out[name].dtype))
    for name, factor in factors.items():
        out[name] = (out[name] * factor).astype(out[name].dtype)
    return out
```

```python
from contextlib import ExitStack

import numpy as np

import concourse.bass as bass
from concourse import mybir

F32 = mybir.dt.float32
BF16 = mybir.dt.bfloat16
I32 = mybir.dt.int32
ALU = mybir.AluOpType
ACT = mybir.ActivationFunctionType
AX = mybir.AxisListType.X

P = 128
NODES, FEAT = 3125, 128
EDGES, EDIM = 103125, 32
HEADS, CH = 4, 32
NB = -(-NODES // P)
FULL, LAST = NODES // P, NODES % P
TILES = -(-EDGES // P)
KB = -(-TILES // P)
GI = 8
NI = -(-(TILES + NB - 1) // 32) * 32
NG = NI // GI
IB = NI // 32
HALF = NI // 2
IKB = -(-NI // P)
CHUNKS = P // HEADS
CHUNK = NI * P // CHUNKS
BIG = 1.0e37
EPS = 1e-5
PAD_DST = 8191
NGRP = 5
GB = NB // NGRP
assert GB * NGRP == NB and HALF <= 512
IN_RANGE = "the value is a node block or edge tile number that the chip clamped to its table"


class Memory:
    pass


class Sequence:

    def __init__(self, engine, sem):
        self.engine, self.sem, self.n, self.static = engine, sem, 0, 0

    def did(self, instruction):
        instruction.then_inc(self.sem, 1)
        self.n = self.n + 1
        self.static += 1

    def wait(self):
        self.engine.wait_ge(self.sem, self.n)

    def link(self, instruction):
        self.did(instruction)
        self.wait()

    def enter(self, i, per_step):
        self.start, self.per_step, self.before = self.n, per_step, self.static
        self.n = self.start + i * per_step

    def leave(self, steps):
        assert self.static - self.before == self.per_step, self.static - self.before
        self.n = self.start + steps * self.per_step


def loads(nc, engine, row, first, count, top):
    _, values = nc.values_load_multi_w_load_instructions(
        row[0:1, bass.ds(first, count)], engines=[engine.engine], min_val=0, max_val=top,
        skip_runtime_bounds_check_because=IN_RANGE)
    return values


def node_bank(m, n, block):
    return m.ps[:, 2 * (n % 2) + block // 4, (block % 4) * P:(block % 4 + 1) * P]


def node_group(m, n):
    flat = m.ps[:, 2 * (n % 2):2 * (n % 2) + 2, :].rearrange("p k n -> p (k n)")
    return flat[:, 0:GB * FEAT].rearrange("p (b f) -> p b f", b=GB)


def group_blocks(g):
    return slice(g * GB, (g + 1) * GB)


def group_cols(g):
    return slice(g * GB * P, (g + 1) * GB * P)



def load_inputs(nc, m, t):
    with ExitStack() as ph:
        def sem(name):
            return ph.enter_context(nc.semaphore(name))

        nodes_in, weights_in, cleared, counted, made = (
            sem(n) for n in ("nodes_in", "weights_in", "cleared", "counted", "made"))
        with nc.Block() as block:
            @block.sync
            def _(sp):
                sp.wait_ge(cleared, 1)
                sp.dma_start(m.X[:, 0:FULL, :],
                             t["x"][0:FULL * P, :].rearrange("(b p) f -> p b f", p=P)).then_inc(nodes_in, 16)
                sp.dma_start(m.X[0:LAST, FULL, :], t["x"][FULL * P:NODES, :]).then_inc(nodes_in, 16)
                sp.wait_ge(nodes_in, 32)

            @block.scalar
            def _(act):
                n = 0
                for name, tile in m.W.items():
                    act.dma_start(tile[:, :], t[name]).then_inc(weights_in, 16)
                    n += 16
                act.dma_start(m.We[:, :], t["We"]).then_inc(weights_in, 16)
                for name, tile in m.brow.items():
                    act.dma_start(tile[0:1, :], t[name].rearrange("(a f) -> a f", a=1)).then_inc(weights_in, 16)
                    n += 16
                for name, tile in (("b1", m.b1col), ("b2", m.b2col)):
                    act.dma_start(tile[:, :], t[name].rearrange("(f a) -> f a", a=1)).then_inc(weights_in, 16)
                for name, tile in (("gamma", m.gamma), ("beta", m.beta)):
                    act.dma_start(tile[:, :], t[name].rearrange("(a f) -> a f", a=1).to_broadcast([P, FEAT]))\
                       .then_inc(weights_in, 16)
                act.wait_ge(weights_in, n + 16 * 5)

            @block.vector
            def _(dve):
                nc.vector.memset(m.X[:, FULL, :], 0.0).then_inc(cleared, 1)
                nc.vector.memset(m.ones[:, :], 1.0)
                nc.vector.memset(m.eps[:, :], EPS)
                dve.wait_ge(counted, 1)
                nc.vector.tensor_copy(m.iota_f[:, :], m.iota_i[:, :]).then_inc(made, 1)
                dve.wait_ge(counted, 5)
                nc.vector.tensor_copy(m.ident16[:, :], m.ident[:, :])
                nc.vector.tensor_copy(m.pid_f[:, :], m.pid_i[:, :])

            @block.gpsimd
            def _(pool):
                pool.iota(m.iota_i[:, :], [[1, NI]], base=0, channel_multiplier=0).then_inc(counted, 1)
                pool.iota(m.pid_i[:, :], [[P, KB + 1]], base=0, channel_multiplier=1).then_inc(counted, 1)
                pool.iota(m.item_i[:, :], [[P, IKB]], base=0, channel_multiplier=1).then_inc(counted, 1)
                pool.memset(m.ident[:, :], 0.0).then_inc(counted, 1)
                pool.wait_ge(counted, 4)
                pool.affine_select(out=m.ident[:, :], in_=m.ident[:, :], compare_op=ALU.not_equal, fill=1.0,
                                   base=0, pattern=[[-1, P]], channel_multiplier=1).then_inc(counted, 1)



def list_items(nc, m, t):
    with ExitStack() as ph:
        def sb(name, shape, dt=F32):
            return ph.enter_context(nc.sbuf_tensor(name, shape, dt))

        def sem(name):
            return ph.enter_context(nc.semaphore(name))

        sel = sb("sel", [P, KB, NI])
        raw = [sb(f"raw_{n}", [P, KB, P], I32) for n in ("src", "dst", "prev", "next")]
        src_f, dst_f, first_f, last_f = (sb(n, [P, KB, P]) for n in ("src_f", "dst_f", "first_f", "last_f"))
        ends_i = sb("ends_i", [1, 2, TILES], I32)
        block0, length = sb("block0", [1, TILES]), sb("length", [1, TILES])
        row = sb("row", [1, 3, KB * P])
        cols = sb("cols", [P, 3, 8])
        shift_b = sb("shift_b", [P, KB, P])
        block_f = sb("block_f", [P, NI])
        marks = sb("marks", [P, 3, IKB, P])
        block_c = sb("block_c", [P, IKB])
        item_f = sb("item_f", [P, IKB])

        tiles_in, ends_in, row_made, cols_ps, cols_made, sel_made, rows_made, expanded, taken, marked, kept = (
            sem(n) for n in ("tiles_in", "ends_in", "row_made", "cols_ps", "cols_made", "sel_made", "rows_made",
                             "expanded", "expanded_taken", "marked", "marks_kept"))
        dve_seq = sem("list_dve_seq")
        jobs = [(what, h) for what in ("block", "tile", "src", "dst") for h in range(2)]
        jobs += [(what, k) for k in range(IKB) for what in ("block_c", "first", "last", "dst_c")]

        with nc.Block() as block:
            @block.sync
            def _(sp):
                for k, name in enumerate(("first_dst", "last_dst")):
                    sp.dma_start(ends_i[0:1, k, :], t[name].rearrange("(a n) -> a n", a=1)).then_inc(ends_in, 16)
                for k, name in enumerate(("src_rows", "dst_rows", "prev_rows", "next_rows")):
                    sp.dma_start(raw[k][:, :, :], t[name].rearrange("(k p) e -> p k e", p=P)).then_inc(tiles_in, 16)
                sp.wait_ge(marked, 1)
                full = NI // P
                for k in range(3):
                    view = m.marks_dram[k]
                    sp.dma_start(view[0:full * P * P].rearrange("(b p e) -> p b e", p=P, e=P),
                                 marks[:, k, 0:full, :]).then_inc(kept, 16)
                    sp.dma_start(view[full * P * P:NI * P].rearrange("(p e) -> p e", e=P),
                                 marks[0:NI % P, k, full, :]).then_inc(kept, 16)
                sp.wait_ge(kept, 16 * 6)

            @block.vector
            def _(dve):
                seq = Sequence(dve, dve_seq)
                dve.wait_ge(ends_in, 32)
                seq.did(nc.vector.memset(row[:, :, :], 0.0))
                seq.link(nc.vector.tensor_single_scalar(ends_i[:, :, :], ends_i[:, :, :], 7, ALU.arith_shift_right))
                seq.did(nc.vector.tensor_copy(block0[:, :], ends_i[0:1, 0, :]))
                seq.did(nc.vector.tensor_copy(length[:, :], ends_i[0:1, 1, :]))
                seq.wait()
                seq.link(nc.vector.tensor_tensor(length[:, :], length[:, :], block0[:, :], ALU.subtract))
                seq.link(nc.vector.tensor_scalar_add(length[:, :], length[:, :], 1.0))
                seq.link(nc.vector.tensor_tensor_scan(row[0:1, 1, 0:TILES], length[:, :], length[:, :], 0.0,
                                                      ALU.add, ALU.max))
                seq.link(nc.vector.tensor_tensor(row[0:1, 0, 0:TILES], row[0:1, 1, 0:TILES], length[:, :],
                                                 ALU.subtract))
                seq.link(nc.vector.tensor_tensor(row[0:1, 2, 0:TILES], block0[:, :], row[0:1, 0, 0:TILES],
                                                 ALU.subtract))
                nc.vector.tensor_copy(item_f[:, :], m.item_i[:, :]).then_inc(row_made, 1)
                dve.wait_ge(cols_ps, 1)
                nc.vector.tensor_copy(cols[:, :, :], m.ps[:, 7, 0:24].rearrange("p (a k) -> p a k", a=3))\
                    .then_inc(cols_made, 1)
                dve.wait_ge(cols_made, 1)
                for k in range(KB):
                    seq.link(nc.vector.tensor_scalar(sel[:, k, :], m.iota_f[:, :], cols[:, 0, k:k + 1], None,
                                                     ALU.is_ge))
                    seq.did(nc.vector.tensor_copy(shift_b[:, k, :], cols[:, 2, k:k + 1].to_broadcast([P, P])))
                    seq.link(nc.vector.scalar_tensor_tensor(sel[:, k, :], m.iota_f[:, :], cols[:, 1, k:k + 1],
                                                            sel[:, k, :], ALU.is_lt, ALU.mult))
                nc.vector.tensor_copy(block_c[:, :], item_f[:, :]).then_inc(sel_made, 1)
                dve.wait_ge(tiles_in, 64)
                seq.did(nc.vector.tensor_copy(src_f[:, :, :], raw[0][:, :, :]))
                seq.did(nc.vector.tensor_copy(dst_f[:, :, :], raw[1][:, :, :]))
                seq.did(nc.vector.tensor_tensor(first_f[:, :, :], raw[1][:, :, :], raw[2][:, :, :], ALU.not_equal))
                nc.vector.tensor_tensor(last_f[:, :, :], raw[1][:, :, :], raw[3][:, :, :], ALU.not_equal)\
                    .then_inc(rows_made, 1)
                seq.wait()
                for n, (what, k) in enumerate(jobs):
                    dve.wait_ge(expanded, n + 1)
                    half = slice(k * HALF, (k + 1) * HALF)
                    got = m.ps[:, n % 4, 0:HALF]
                    rows = min(P, NI - k * P) if k < IKB else P
                    if what == "block":
                        seq.link(nc.vector.tensor_tensor(block_f[:, half], got, m.iota_f[:, half], ALU.add))
                        seq.link(nc.vector.tensor_scalar_min(block_f[:, half], block_f[:, half], float(NB - 1)))
                        last = nc.vector.tensor_copy(m.block_row[0:1, half], block_f[0:1, half])
                    elif what == "tile":
                        last = nc.vector.tensor_copy(m.tile_row[0:1, half], got[0:1, :])
                    elif what == "src":
                        last = nc.vector.tensor_copy(m.idx[:, half], got)
                    elif what == "dst":
                        last = nc.vector.scalar_tensor_tensor(m.rel[:, half], block_f[:, half], -float(P), got,
                                                              ALU.mult, ALU.add)
                    elif what == "block_c":
                        c = slice(k, k + 1)
                        seq.link(nc.vector.tensor_tensor(block_c[0:rows, c], m.ps[0:rows, n % 4, 0:1],
                                                         item_f[0:rows, c], ALU.add))
                        seq.link(nc.vector.tensor_scalar_min(block_c[0:rows, c], block_c[0:rows, c],
                                                             float(NB - 1)))
                        last = nc.vector.tensor_scalar(block_c[0:rows, c], block_c[0:rows, c], float(P), None,
                                                       ALU.mult)
                    elif what == "dst_c":
                        z = marks[0:rows, 2, k, :]
                        seq.link(nc.vector.tensor_scalar(z, m.ps[0:rows, n % 4, 0:P], block_c[0:rows, k:k + 1],
                                                         63.5, ALU.subtract, ALU.subtract))
                        seq.link(nc.vector.tensor_tensor(z, z, z, ALU.mult))
                        last = nc.vector.tensor_scalar(z, z, 64.0 * 64.0, -BIG, ALU.is_gt, ALU.mult)
                    else:
                        last = nc.vector.tensor_scalar(marks[0:rows, ("first", "last").index(what), k, :],
                                                       m.ps[0:rows, n % 4, 0:P], -BIG, None, ALU.mult)
                    last.then_inc(taken, 1)
                    dve.wait_ge(taken, n + 1)
                nc.vector.memset(cols[:, :, :], 0.0).then_inc(marked, 1)

            @block.tensor
            def _(pe):
                pe.wait_ge(row_made, 1)
                for a in range(3):
                    for k in range(KB):
                        last = nc.tensor.matmul(m.ps[:, 7, a * 8 + k:a * 8 + k + 1],
                                                row[0:1, a, k * P:(k + 1) * P], m.ones[0:1, 0:1],
                                                start=True, stop=True)
                last = nc.tensor.matmul(m.ps[:, 7, 7:8], row[0:1, 0, 0:P], m.ones[0:1, 0:1], start=True, stop=True)
                for a in (1, 2):
                    last = nc.tensor.matmul(m.ps[:, 7, a * 8 + 7:a * 8 + 8], row[0:1, a, 0:P], m.ones[0:1, 0:1],
                                            start=True, stop=True)
                last.then_inc(cols_ps, 1)
                pe.wait_ge(sel_made, 1)
                pe.wait_ge(rows_made, 1)
                for n, (what, k) in enumerate(jobs):
                    if n >= 4:
                        pe.wait_ge(taken, n - 3)
                    for kk in range(KB):
                        edge = dict(start=kk == 0, stop=kk == KB - 1)
                        if what in ("block", "tile", "src", "dst"):
                            rhs = sel[:, kk, k * HALF:(k + 1) * HALF]
                            if what == "tile":
                                last = nc.tensor.matmul(m.ps[0:1, n % 4, 0:HALF], m.pid_f[:, kk:kk + 1], rhs, **edge)
                            else:
                                lhsT = dict(block=shift_b, src=src_f, dst=dst_f)[what][:, kk, :]
                                last = nc.tensor.matmul(m.ps[:, n % 4, 0:HALF], lhsT, rhs, **edge)
                        else:
                            rows = min(P, NI - k * P)
                            lhsT = sel[:, kk, k * P:k * P + rows]
                            rhs = dict(block_c=cols[:, 2, kk:kk + 1], first=first_f[:, kk, :],
                                       last=last_f[:, kk, :], dst_c=dst_f[:, kk, :])[what]
                            width = 1 if what == "block_c" else P
                            last = nc.tensor.matmul(m.ps[0:rows, n % 4, 0:width], lhsT, rhs, **edge)
                    last.then_inc(expanded, 1)



def count_degrees(nc, m, t):
    TG = 13
    STEPS = TILES // TG
    assert TG * STEPS == TILES
    with ExitStack() as ph:
        def sb(name, shape, dt=F32):
            return ph.enter_context(nc.sbuf_tensor(name, shape, dt))

        def sem(name):
            return ph.enter_context(nc.semaphore(name))

        node_i = [sb(f"node_i{k}", [P, TILES], I32) for k in range(2)]
        part_i = sb("part_i", [P, TILES], I32)
        low = [sb(f"low{k}", [P, TILES]) for k in range(2)]
        high = [sb(f"high{k}", [P, TILES]) for k in range(2)]
        hot_low = sb("hot_low", [P, 2, TG, P], BF16)
        hot_high = sb("hot_high", [P, 2, TG, NB], BF16)
        cols_in, seq_sem, hot, counted, added = (
            sem(n) for n in ("edge_cols_in", "deg_dve_seq", "hot_made", "counted_tiles", "degrees_added"))
        act_seq = sem("deg_act")
        with nc.Block() as block:
            @block.sync
            def _(sp):
                for k, name in enumerate(("dst_cols", "src_cols")):
                    sp.dma_start(node_i[k][:, :], t[name]).then_inc(cols_in, 16)

            @block.vector
            def _(dve):
                seq = Sequence(dve, seq_sem)
                for deg in (m.deg_in, m.deg_out):
                    seq.did(nc.vector.memset(deg[:, :], 0.0))
                dve.wait_ge(cols_in, 32)
                for k in range(2):
                    seq.link(nc.vector.tensor_single_scalar(part_i[:, :], node_i[k][:, :], 127, ALU.bitwise_and))
                    seq.link(nc.vector.tensor_copy(low[k][:, :], part_i[:, :]))
                    seq.link(nc.vector.tensor_single_scalar(part_i[:, :], node_i[k][:, :], 7,
                                                            ALU.arith_shift_right))
                    seq.link(nc.vector.tensor_copy(high[k][:, :], part_i[:, :]))
                with dve.Fori(0, STEPS) as i:
                    for k in range(2):
                        dve.wait_ge(counted, i * 2 + k + 1)
                        cols = bass.ds(i * TG, TG)
                        for out, width, part in ((hot_low, P, low), (hot_high, NB, high)):
                            last = nc.vector.tensor_tensor(
                                out[:, k, :, :],
                                m.iota_f[:, 0:width].rearrange("p (a w) -> p a w", a=1).to_broadcast([P, TG, width]),
                                part[k][:, cols].rearrange("p (t a) -> p t a", a=1).to_broadcast([P, TG, width]),
                                ALU.is_equal)
                            last.then_inc(hot, 1)
                        dve.wait_ge(counted, i * 2 + k + 3)
                        deg = (m.deg_in, m.deg_out)[k]
                        nc.vector.tensor_tensor(deg[:, :], deg[:, :], m.ps[:, k, 0:NB], ALU.add).then_inc(added, 1)
                        dve.wait_ge(added, i * 2 + k + 1)
                for deg, out in ((m.deg_in, m.rcnt), (m.deg_in, m.isq_in), (m.deg_out, m.isq_out)):
                    seq.link(nc.vector.tensor_scalar_max(out[:, :], deg[:, :], 1.0))
                nc.vector.reciprocal(m.rcnt[:, :], m.rcnt[:, :]).then_inc(act_seq, 1)
                dve.wait_ge(act_seq, 3)
                for out in (m.isq_in, m.isq_out):
                    seq.did(nc.vector.reciprocal(out[:, :], out[:, :]))
                seq.wait()

            @block.scalar
            def _(act):
                act.wait_ge(act_seq, 1)
                for out in (m.isq_in, m.isq_out):
                    act.activation(out[:, :], out[:, :], ACT.Sqrt).then_inc(act_seq, 1)

            @block.tensor
            def _(pe):
                pe.sem_inc(counted, 2)
                with pe.Fori(0, STEPS) as i:
                    for k in range(2):
                        pe.wait_ge(hot, i * 4 + 2 * k + 2)
                        for j in range(TG):
                            last = nc.tensor.matmul(m.ps[:, k, 0:NB], hot_low[:, k, j, :], hot_high[:, k, j, :],
                                                    start=j == 0, stop=j == TG - 1)
                        last.then_inc(counted, 1)



def normalise(nc, m, name, again=False):
    with ExitStack() as ph:
        def sb(n, shape, dt=F32):
            return ph.enter_context(nc.sbuf_tensor(f"{name}_{n}", shape, dt))

        def sem(n):
            return ph.enter_context(nc.semaphore(f"{name}_{n}"))

        stats, moments = sb("stats", [P, NB, 6]), sb("moments", [P, NB, 2])
        std = sb("std", [P, NB])
        seq_sem, var_made, std_made, centred, relu_made = (
            sem(n) for n in ("dve_seq", "var_made", "std_made", "centred", "relu_made"))
        rows_made, rows_kept, T_ps, T_taken = (sem(n) for n in ("rows_made", "rows_kept", "T_ps", "T_taken"))

        passes = 2 if again else 1
        rows = m.D if again else m.H
        with nc.Block() as block:
            @block.vector
            def _(dve):
                seq = Sequence(dve, seq_sem)
                for n in range(passes):
                    source = m.H if n else m.X
                    if n:
                        dve.wait_ge(relu_made, NGRP)
                    for b in range(NB):
                        seq.did(nc.vector.bn_stats(stats[:, b, :], source[:, b, :]))
                    seq.wait()
                    for b in range(NB):
                        seq.did(nc.vector.bn_aggr(moments[:, b, :], stats[:, b, :]))
                    seq.wait()
                    seq.link(nc.vector.tensor_copy(m.rstd[:, :], moments[:, :, 1]))
                    nc.vector.tensor_copy(std[:, :], m.rstd[:, :]).then_inc(var_made, 1)
                    dve.wait_ge(std_made, n + 1)
                    seq.link(nc.vector.reciprocal(m.rstd[:, :], std[:, :]))
                    for g in range(NGRP):
                        for b in range(g * GB, (g + 1) * GB):
                            last = nc.vector.tensor_scalar(m.D[:, b, :], source[:, b, :], moments[:, b, 0:1],
                                                           m.rstd[:, b:b + 1], ALU.subtract, ALU.mult)
                        last.then_inc(centred, 1)
                if again:
                    for g in range(NGRP):
                        dve.wait_ge(centred, NGRP + g + 1)
                        blocks = group_blocks(g)
                        bc = [v[:, :].rearrange("p (a f) -> p a f", a=1).to_broadcast([P, GB, FEAT])
                              for v in (m.gamma, m.beta)]
                        seq.link(nc.vector.tensor_tensor(m.D[:, blocks, :], m.D[:, blocks, :], bc[0], ALU.mult))
                        seq.link(nc.vector.tensor_tensor(m.H[:, blocks, :], m.D[:, blocks, :], bc[1], ALU.add))
                        for b in range(g * GB, (g + 1) * GB):
                            last = nc.vector.tensor_scalar(m.D[:, b, :], m.H[:, b, :], m.isq_out[:, b:b + 1], None,
                                                           ALU.mult)
                        last.then_inc(rows_made, 1)

            @block.scalar
            def _(act):
                for n in range(passes):
                    act.wait_ge(var_made, n + 1)
                    act.activation(std[:, :], std[:, :], ACT.Sqrt, bias=m.eps[:, 0:1]).then_inc(std_made, 1)
                    for g in range(NGRP if n == 0 else 0):
                        act.wait_ge(centred, g + 1)
                        act.activation(m.H[:, group_blocks(g), :], m.D[:, group_blocks(g), :], ACT.Relu)\
                           .then_inc(relu_made if again else rows_made, 1)
                        if again:
                            act.wait_ge(relu_made, g + 1)
                for g in range(NGRP):
                    act.wait_ge(T_ps, g + 1)
                    act.activation(m.HT[:, group_cols(g)].rearrange("p (b f) -> p b f", b=GB), node_group(m, g),
                                   ACT.Copy).then_inc(T_taken, 1)

            @block.sync
            def _(sp):
                for g in range(NGRP):
                    sp.wait_ge(rows_made, g + 1)
                    sp.dma_start(m.h_table[g * GB * P:(g + 1) * GB * P, :].rearrange("(b p) f -> p b f", p=P),
                                 rows[:, group_blocks(g), :]).then_inc(rows_kept, 16)
                sp.wait_ge(rows_kept, 16 * NGRP)

            @block.tensor
            def _(pe):
                for g in range(NGRP):
                    pe.wait_ge(rows_made, g + 1)
                    if g >= 2:
                        pe.wait_ge(T_taken, g - 1)
                    for b in range(GB):
                        last = nc.tensor.transpose(node_bank(m, g, b), m.H[:, g * GB + b, :], m.ident[:, :])
                    last.then_inc(T_ps, 1)



def sum_neighbours(nc, m, name):
    with ExitStack() as ph:
        def sb(n, shape, dt=F32):
            return ph.enter_context(nc.sbuf_tensor(f"{name}_{n}", shape, dt))

        def sem(n):
            return ph.enter_context(nc.semaphore(f"{name}_{n}"))

        got, hot = sb("got", [P, 2, GI, FEAT]), sb("hot", [P, 2, GI, P])
        idx_now = sb("idx_now", [P, 2, GI], I32)
        idx_staged, hot_made, summed, added, turns = (
            sem(n) for n in ("idx_staged", "hot_made", "summed", "added", "turns"))
        got_in = [sem(f"got_in{p}") for p in range(2)]
        START = 4
        with nc.Block() as block:
            @block.gpsimd
            def _(pool):
                with pool.Fori(0, NG // 2) as i:
                    for p in range(2):
                        pool.wait_ge(summed, i * 4 + 2 * p + 2)
                        pool.sem_inc(turns, 1)
                        nc.gpsimd.tensor_copy(idx_now[:, p, :], m.idx[:, bass.ds(i * 2 * GI + p * GI, GI)])\
                            .then_inc(idx_staged, 1)
                        pool.wait_ge(idx_staged, i * 2 + p + 1)
                        pool.sem_inc(turns, 1)
                        for j in range(GI):
                            pool.indirect_dma_start(
                                out=got[:, p, j, :], out_offset=None, in_=m.h_table[:, :],
                                in_offset=bass.IndirectOffsetOnAxis(ap=idx_now[:, p, j:j + 1], axis=0))\
                                .then_inc(got_in[p], 16)

            @block.vector
            def _(dve):
                nc.vector.memset(m.AGGT[:, :], 0.0).then_inc(added, 8)
                with dve.Fori(0, NG // 2) as i:
                    for p in range(2):
                        blocks = loads(nc, dve, m.block_row, i * 2 * GI + p * GI, GI, NB - 1)
                        dve.wait_ge(summed, i * 4 + 2 * p + 2)
                        nc.vector.tensor_tensor(
                            hot[:, p, :, :],
                            m.iota_f[:, 0:P].rearrange("p (a w) -> p a w", a=1).to_broadcast([P, GI, P]),
                            m.rel[:, bass.ds(i * 2 * GI + p * GI, GI)].rearrange("p (t a) -> p t a", a=1)
                            .to_broadcast([P, GI, P]), ALU.is_equal).then_inc(hot_made, 1)
                        for half in range(2):
                            dve.wait_ge(summed, START + i * 4 + 2 * p + half + 1)
                            for j in range(4):
                                done = i * 2 * GI + p * GI + half * 4 + j
                                dve.wait_ge(added, 8 + done)
                                cols = bass.ds(blocks[half * 4 + j] * P, P)
                                nc.vector.tensor_tensor(m.AGGT[:, cols], m.AGGT[:, cols],
                                                        m.ps[:, 4 + half, j * P:(j + 1) * P], ALU.add)\
                                    .then_inc(added, 1)

            @block.tensor
            def _(pe):
                pe.sem_inc(summed, START)
                with pe.Fori(0, NG // 2) as i:
                    for p in range(2):
                        pe.wait_ge(hot_made, i * 2 + p + 1)
                        pe.wait_ge(got_in[p], (i + 1) * 16 * GI)
                        for half in range(2):
                            pe.wait_ge(added, i * 2 * GI + p * GI + 4 * (half + 1))
                            for j in range(4):
                                last = nc.tensor.matmul(m.ps[:, 4 + half, j * P:(j + 1) * P],
                                                        got[:, p, half * 4 + j, :], hot[:, p, half * 4 + j, :],
                                                        start=True, stop=True)
                            last.then_inc(summed, 1)



def project_pair(nc, m, name, self_w, agg_w, bias, scale):
    with ExitStack() as ph:
        def sem(n):
            return ph.enter_context(nc.semaphore(f"{name}_{n}"))

        product, taken = sem("product"), sem("taken")
        with nc.Block() as block:
            @block.tensor
            def _(pe):
                for n in range(2 * NGRP):
                    g = n // 2
                    if n >= 2:
                        pe.wait_ge(taken, n - 1)
                    for b in range(GB):
                        cols = slice((g * GB + b) * P, (g * GB + b + 1) * P)
                        if n % 2 == 0:
                            nc.tensor.matmul(node_bank(m, n, b), m.HT[:, cols], self_w[:, :], start=True, stop=False)
                            last = nc.tensor.matmul(node_bank(m, n, b), m.ones[0:1, :], bias[0:1, :],
                                                    start=False, stop=True)
                        else:
                            last = nc.tensor.matmul(node_bank(m, n, b), m.AGGT[:, cols], agg_w[:, :],
                                                    start=True, stop=True)
                    last.then_inc(product, 1)

            @block.vector
            def _(dve):
                for n in range(2 * NGRP):
                    g = n // 2
                    dve.wait_ge(product, n + 1)
                    if n % 2 == 0:
                        blocks = group_blocks(g)
                        nc.vector.tensor_tensor(m.X[:, blocks, :], m.X[:, blocks, :], node_group(m, n), ALU.add)\
                            .then_inc(taken, 1)
                        dve.wait_ge(taken, n + 1)
                    else:
                        for b in range(GB):
                            at = g * GB + b
                            last = nc.vector.scalar_tensor_tensor(m.X[:, at, :], node_bank(m, n, b),
                                                                  scale[:, at:at + 1], m.X[:, at, :],
                                                                  ALU.mult, ALU.add)
                        last.then_inc(taken, 1)


def project_sum(nc, m):
    with ExitStack() as ph:
        def sem(n):
            return ph.enter_context(nc.semaphore(f"l1_{n}"))

        summed, product, taken = sem("summed"), sem("product"), sem("taken")
        with nc.Block() as block:
            @block.gpsimd
            def _(pool):
                for g in range(NGRP):
                    nc.gpsimd.tensor_tensor(m.HT[:, group_cols(g)], m.HT[:, group_cols(g)], m.AGGT[:, group_cols(g)],
                                            ALU.add).then_inc(summed, 1)

            @block.tensor
            def _(pe):
                for g in range(NGRP):
                    pe.wait_ge(summed, g + 1)
                    if g >= 2:
                        pe.wait_ge(taken, g - 1)
                    for b in range(GB):
                        cols = slice((g * GB + b) * P, (g * GB + b + 1) * P)
                        last = nc.tensor.matmul(node_bank(m, g, b), m.HT[:, cols], m.W["W1"][:, :],
                                                start=True, stop=True)
                    last.then_inc(product, 1)

            @block.vector
            def _(dve):
                for g in range(NGRP):
                    dve.wait_ge(product, g + 1)
                    blocks = group_blocks(g)
                    nc.vector.scalar_tensor_tensor(m.X[:, blocks, :], node_group(m, g), 0.0, m.X[:, blocks, :],
                                                   ALU.max, ALU.add).then_inc(taken, 1)



def project_qkv(nc, m, Q3):
    with ExitStack() as ph:
        def sem(n):
            return ph.enter_context(nc.semaphore(f"qkv_{n}"))

        kv_rows = ph.enter_context(nc.sbuf_tensor("kv_rows", [P, 2, GB, 2, FEAT], F32))
        q_rest = ph.enter_context(nc.sbuf_tensor("q_rest", [P, GB, FEAT], F32))
        product, q_taken, kv_taken, seq_sem = (sem(n) for n in ("product", "q_taken", "kv_taken", "dve_seq"))
        kept = [sem(f"kv_kept{p}") for p in range(2)]
        names = ("k", "v", "q")
        with nc.Block() as block:
            @block.tensor
            def _(pe):
                for n in range(3 * NGRP):
                    g, what = n // 3, names[n % 3]
                    if n >= 2:
                        before = n - 2
                        if before % 3 == 2:
                            pe.wait_ge(q_taken, before // 3 + 1)
                        else:
                            pe.wait_ge(kv_taken, before // 3 * 2 + before % 3 + 1)
                    for b in range(GB):
                        cols = slice((g * GB + b) * P, (g * GB + b + 1) * P)
                        nc.tensor.matmul(node_bank(m, n, b), m.HT[:, cols], m.W["W" + what][:, :],
                                         start=True, stop=False)
                        last = nc.tensor.matmul(node_bank(m, n, b), m.ones[0:1, :], m.brow["b" + what][0:1, :],
                                                start=False, stop=True)
                    last.then_inc(product, 1)

            @block.scalar
            def _(act):
                for g in range(NGRP):
                    if g >= 2:
                        act.wait_ge(kept[g % 2], 16 * (g // 2))
                    for k in range(2):
                        act.wait_ge(product, 3 * g + k + 1)
                        act.activation(kv_rows[:, g % 2, :, k, :], node_group(m, 3 * g + k), ACT.Copy)\
                           .then_inc(kv_taken, 1)

            @block.sync
            def _(sp):
                for g in range(NGRP):
                    sp.wait_ge(kv_taken, 2 * g + 2)
                    sp.dma_start(m.kv_table[g * GB * P:(g + 1) * GB * P, :].rearrange("(b p) f -> p b f", p=P),
                                 kv_rows[:, g % 2, :, :, :].rearrange("p b k f -> p b (k f)"))\
                        .then_inc(kept[g % 2], 16)
                sp.wait_ge(kept[0], 16 * ((NGRP + 1) // 2))
                sp.wait_ge(kept[1], 16 * (NGRP // 2))

            @block.vector
            def _(dve):
                seq = Sequence(dve, seq_sem)
                for g in range(NGRP):
                    dve.wait_ge(product, 3 * g + 3)
                    q = node_group(m, 3 * g + 2)
                    parts = [Q3[:, group_blocks(g), k, :] for k in range(3)]
                    seq.link(nc.vector.tensor_copy(parts[0], q))
                    nc.vector.tensor_tensor(q_rest[:, :, :], q, parts[0], ALU.subtract).then_inc(q_taken, 1)
                    dve.wait_ge(q_taken, g + 1)
                    seq.link(nc.vector.tensor_copy(parts[1], q_rest[:, :, :]))
                    seq.link(nc.vector.tensor_tensor(q_rest[:, :, :], q_rest[:, :, :], parts[1], ALU.subtract))
                    seq.link(nc.vector.tensor_copy(parts[2], q_rest[:, :, :]))


def score_edges(nc, m, Q3):
    GL = 4
    with ExitStack() as ph:
        def sb(n, shape, dt=F32):
            return ph.enter_context(nc.sbuf_tensor(f"sc_{n}", shape, dt))

        def sem(n):
            return ph.enter_context(nc.semaphore(f"sc_{n}"))

        kv, ea = sb("kv", [P, 2, GI, 2, FEAT]), sb("ea", [EDIM, 2, GI, P])
        idx_now = sb("idx_now", [P, 2, GI], I32)
        hot, hotT = sb("hot", [P, 2, GI, P], BF16), sb("hotT", [P, 2, GI, P], BF16)
        prod = sb("prod", [P, 2, 4, FEAT])
        hotT_ps = m.ps16
        turns, idx_staged, hot_made, turned, hotT_made, terms, edged, multiplied, scored = (
            sem(n) for n in ("turns", "idx_staged", "hot_made", "turned", "hotT_made", "terms", "edged", "multiplied",
                             "scored"))
        kv_in, ea_in, spilled = ([sem(f"{n}{p}") for p in range(2)] for n in ("kv_in", "ea_in", "spilled"))
        STEPS = NG // GL
        with nc.Block() as block:
            @block.gpsimd
            def _(pool):
                with pool.Fori(0, STEPS) as i:
                    for q in range(GL):
                        p = q % 2
                        pool.wait_ge(spilled[p], i * (GL // 2 * 16) + q // 2 * 16 + 16)
                        pool.sem_inc(turns, 1)
                        nc.gpsimd.tensor_copy(idx_now[:, p, :], m.idx[:, bass.ds(i * GL * GI + q * GI, GI)])\
                            .then_inc(idx_staged, 1)
                        pool.wait_ge(idx_staged, i * GL + q + 1)
                        pool.sem_inc(turns, 1)
                        for j in range(GI):
                            pool.indirect_dma_start(
                                out=kv[:, p, j, :, :].rearrange("p k f -> p (k f)"), out_offset=None,
                                in_=m.kv_table[:, :],
                                in_offset=bass.IndirectOffsetOnAxis(ap=idx_now[:, p, j:j + 1], axis=0))\
                                .then_inc(kv_in[p], 16)

            @block.scalar
            def _(act):
                with act.Fori(0, STEPS) as i:
                    for q in range(GL):
                        p = q % 2
                        tiles = loads(nc, act, m.tile_row, i * GL * GI + q * GI, GI, TILES - 1)
                        act.wait_ge(terms, i * GL * 2 + 2 * q + 2)
                        for j in range(GI):
                            act.dma_start(ea[:, p, j, :], m.ea_tiles[bass.ds(tiles[j], 1), :, :]
                                          .rearrange("a c e -> (a c) e")).then_inc(ea_in[p], 16)
                        act.wait_ge(turned, i * GL + q + 3)
                        act.activation(hotT[:, p, :, :], hotT_ps[:, p, :].rearrange("p (j e) -> p j e", j=GI),
                                       ACT.Copy).then_inc(hotT_made, 1)

            @block.vector
            def _(dve):
                with dve.Fori(0, STEPS) as i:
                    for q in range(GL):
                        p = q % 2
                        dve.wait_ge(turned, i * GL + q + 1)
                        nc.vector.tensor_tensor(
                            hot[:, p, :, :],
                            m.iota_f[:, 0:P].rearrange("p (a w) -> p a w", a=1).to_broadcast([P, GI, P]),
                            m.rel[:, bass.ds(i * GL * GI + q * GI, GI)].rearrange("p (t a) -> p t a", a=1)
                            .to_broadcast([P, GI, P]), ALU.is_equal).then_inc(hot_made, 1)
                        dve.wait_ge(kv_in[p], i * (GL // 2 * 16 * GI) + (q // 2 + 1) * 16 * GI)
                        for half in range(2):
                            n = i * GL * 2 + 2 * q + half
                            js = slice(4 * half, 4 * half + 4)
                            dve.wait_ge(terms, n + 5)
                            e = m.ps[:, 4 + half, :].rearrange("p (j a f) -> p j a f", j=4, a=1)\
                                .to_broadcast([P, 4, 2, FEAT])
                            nc.vector.tensor_tensor(kv[:, p, js, :, :], kv[:, p, js, :, :], e, ALU.add)\
                                .then_inc(edged, 1)
                            dve.wait_ge(edged, n + 1)
                            nc.vector.tensor_tensor(
                                prod[:, half, :, :], kv[:, p, js, 0, :],
                                m.ps[:, 2 + half, :].rearrange("p (j f) -> p j f", j=4), ALU.mult)\
                                .then_inc(multiplied, 1)
                            dve.wait_ge(multiplied, n + 3)
                            at = m.ALPHA[:, bass.ds(i, 1), :, q * GI + 4 * half:q * GI + 4 * half + 4]
                            nc.vector.tensor_reduce(
                                at.rearrange("p a h j -> p j (a h)"),
                                prod[:, half, :, :].rearrange("p j (h c) -> p j h c", h=HEADS), AX, ALU.add)\
                                .then_inc(scored, 1)
                            dve.wait_ge(scored, n + 1)

            @block.sync
            def _(sp):
                for p in range(2):
                    sp.sem_inc(spilled[p], 16)
                with sp.Fori(0, NG // 2) as i:
                    for p in range(2):
                        sp.wait_ge(multiplied, i * 4 + 2 * p + 4)
                        sp.dma_start(m.vj_spill[bass.ds(i * 2 + p, 1), :, :]
                                     .rearrange("a p (j f) -> (a p) j f", j=GI), kv[:, p, :, 1, :])\
                            .then_inc(spilled[p], 16)
                for p in range(2):
                    sp.wait_ge(spilled[p], NG // 2 * 16 + 16)

            @block.tensor
            def _(pe):
                pe.sem_inc(turned, 2)
                pe.sem_inc(terms, 4)
                pe.sem_inc(hotT_made, 2)
                pe.sem_inc(multiplied, 2)
                with pe.Fori(0, STEPS) as i:
                    for q in range(GL):
                        p = q % 2
                        blocks = loads(nc, pe, m.block_row, i * GL * GI + q * GI, GI, NB - 1)
                        pe.wait_ge(hot_made, i * GL + q + 1)
                        pe.wait_ge(hotT_made, i * GL + q + 1)
                        for j in range(GI):
                            last = nc.tensor.transpose(hotT_ps[:, p, j * P:(j + 1) * P], hot[:, p, j, :],
                                                       m.ident16[:, :])
                        last.then_inc(turned, 1)
                        pe.wait_ge(ea_in[p], i * (GL // 2 * 16 * GI) + (q // 2 + 1) * 16 * GI)
                        pe.wait_ge(hotT_made, i * GL + q + 3)
                        for half in range(2):
                            pe.wait_ge(multiplied, i * GL * 2 + 2 * q + half + 1)
                            for j in range(4):
                                jj = 4 * half + j
                                cols = slice(j * P, (j + 1) * P)
                                nc.tensor.matmul(m.ps[:, 4 + half, cols], ea[:, p, jj, :], m.We[:, :],
                                                 start=True, stop=True)
                                for k in range(3):
                                    last = nc.tensor.matmul(
                                        m.ps[:, 2 + half, cols], hotT[:, p, jj, :],
                                        Q3[:, bass.ds(blocks[jj], 1), k, :].rearrange("p a f -> p (a f)"),
                                        start=k == 0, stop=k == 2)
                            last.then_inc(terms, 1)


def transpose_blocks(nc, m, pe, source, ready, taken, identity):
    groups = -(-IB // 4)
    for g in range(groups):
        if g >= 4:
            pe.wait_ge(taken, g - 3)
        for b in range(g * 4, min(g * 4 + 4, IB)):
            last = nc.tensor.transpose(m.ps[:, g % 4, (b % 4) * P:(b % 4 + 1) * P], source(b), identity)
        last.then_inc(ready, 1)


def softmax_edges(nc, m):
    with ExitStack() as ph:
        def sb(n, shape, dt=F32):
            return ph.enter_context(nc.sbuf_tensor(f"sm_{n}", shape, dt))

        def sem(n):
            return ph.enter_context(nc.semaphore(f"sm_{n}"))

        turned = sb("turned", [P, IB, P])
        chunk, invalid = sb("chunk", [P, CHUNK]), sb("invalid", [P, CHUNK])
        marks = [sb(n, [P, CHUNK]) for n in ("first", "last")]
        best = [sb(n, [P, CHUNK]) for n in ("forward", "backward")]
        ends = sb("ends", [P, 2, 2])
        end_rows = sb("end_rows", [1, 4, P])
        carry_rows = sb("carry_rows", [1, 2, P])
        carry = sb("carry", [P, 2])
        T_ps, T_taken, T_out, alpha_in, marks_in, seq_sem = (
            sem(n) for n in ("T_ps", "T_taken", "T_out", "alpha_in", "marks_in", "dve_seq"))
        ends_made, ends_ps, carry_made, carry_ps, maxed, exp_made, exp_out, exp_in, back_ps, back_taken = (
            sem(n) for n in ("ends_made", "ends_ps", "carry_made", "carry_ps", "maxed", "exp_made", "exp_out",
                             "exp_in", "back_ps", "back_taken"))
        groups = -(-IB // 4)

        def bank(g):
            n = min(4, IB - g * 4)
            return m.ps[:, g % 4, 0:n * P].rearrange("p (b e) -> p b e", b=n), slice(g * 4, g * 4 + n)

        def by_item(dram_row):
            return dram_row.rearrange("(b i e) -> i b e", i=32, e=P)

        with nc.Block() as block:
            @block.tensor
            def _(pe):
                transpose_blocks(nc, m, pe, lambda b: m.ALPHA[:, b, :, :].rearrange("p h i -> p (h i)"),
                                 T_ps, T_taken, m.ident[:, :])
                pe.wait_ge(ends_made, 1)
                for k in range(4):
                    last = nc.tensor.transpose(m.ps[0:1, 4, k * P:(k + 1) * P], ends[:, k // 2, k % 2:k % 2 + 1],
                                               m.ident[:, :])
                last.then_inc(ends_ps, 1)
                pe.wait_ge(carry_made, 1)
                for k in range(2):
                    last = nc.tensor.transpose(m.ps[:, 5, k:k + 1], carry_rows[0:1, k, :], m.ident[0:1, 0:1])
                last.then_inc(carry_ps, 1)
                pe.wait_ge(exp_in, 16 * HEADS)
                transpose_blocks(nc, m, pe, lambda b: turned[:, b, :], back_ps, back_taken, m.ident[:, :])

            @block.scalar
            def _(act):
                for g in range(groups):
                    act.wait_ge(T_ps, g + 1)
                    src, blocks = bank(g)
                    act.activation(turned[:, blocks, :], src, ACT.Copy).then_inc(T_taken, 1)
                act.wait_ge(maxed, 1)
                act.activation(chunk[:, :], chunk[:, :], ACT.Exp, scale=float(CH) ** -0.5).then_inc(exp_made, 1)
                for g in range(groups):
                    act.wait_ge(back_ps, g + 1)
                    src, blocks = bank(g)
                    act.activation(m.ALPHA[:, blocks, :, :].rearrange("p b h i -> p b (h i)"), src, ACT.Copy)\
                       .then_inc(back_taken, 1)

            @block.sync
            def _(sp):
                for k, tile in enumerate((*marks, invalid)):
                    for h in range(HEADS):
                        sp.dma_start(tile[h * CHUNKS:(h + 1) * CHUNKS, :],
                                     m.marks_dram[k].rearrange("(c n) -> c n", c=CHUNKS)).then_inc(marks_in, 16)
                sp.wait_ge(T_taken, groups)
                for h in range(HEADS):
                    sp.dma_start(by_item(m.alpha_dram[h]), turned[h * 32:(h + 1) * 32, :, :]).then_inc(T_out, 16)
                sp.wait_ge(T_out, 16 * HEADS)
                sp.dma_start(chunk[:, :], m.alpha_dram.rearrange("h (c n) -> (h c) n", c=CHUNKS))\
                    .then_inc(alpha_in, 16)
                sp.wait_ge(exp_made, 1)
                sp.dma_start(m.ex_dram.rearrange("h (c n) -> (h c) n", c=CHUNKS), chunk[:, :]).then_inc(exp_out, 16)
                sp.wait_ge(exp_out, 16)
                for h in range(HEADS):
                    sp.dma_start(turned[h * 32:(h + 1) * 32, :, :], by_item(m.ex_dram[h])).then_inc(exp_in, 16)

            @block.vector
            def _(dve):
                seq = Sequence(dve, seq_sem)
                dve.wait_ge(marks_in, 16 * 3 * HEADS)
                for k in range(2):
                    seq.did(nc.vector.tensor_reduce(ends[:, k, 1:2], marks[k][:, :], AX, ALU.min))
                seq.did(nc.vector.memset(carry_rows[:, :, :], -BIG))
                dve.wait_ge(alpha_in, 16)
                seq.link(nc.vector.tensor_tensor(chunk[:, :], chunk[:, :], invalid[:, :], ALU.add))

                def scan(k, start):
                    way = slice(None, None, -1) if k else slice(None)
                    return nc.vector.tensor_tensor_scan(best[k][:, way], marks[k][:, way], chunk[:, way], start,
                                                        ALU.add, ALU.max)

                seq.did(scan(0, -BIG))
                seq.link(scan(1, -BIG))
                seq.did(nc.vector.tensor_copy(ends[:, 0, 0:1], best[0][:, CHUNK - 1:CHUNK]))
                nc.vector.tensor_copy(ends[:, 1, 0:1], best[1][:, 0:1]).then_inc(ends_made, 1)
                dve.wait_ge(ends_ps, 1)
                seq.link(nc.vector.tensor_copy(end_rows[:, :, :], m.ps[0:1, 4, :].rearrange("a (k p) -> a k p", k=4)))
                seq.did(nc.vector.memset(end_rows[0:1, 0:2, CHUNKS - 1::CHUNKS], -BIG))
                seq.link(nc.vector.memset(end_rows[0:1, 2:4, 0::CHUNKS], -BIG))
                seq.did(nc.vector.tensor_tensor_scan(carry_rows[0:1, 0, 1:P], end_rows[0:1, 1, 0:P - 1],
                                                     end_rows[0:1, 0, 0:P - 1], -BIG, ALU.add, ALU.max))
                nc.vector.tensor_tensor_scan(carry_rows[0:1, 1, 0:P - 1][:, ::-1], end_rows[0:1, 3, 1:P][:, ::-1],
                                             end_rows[0:1, 2, 1:P][:, ::-1], -BIG, ALU.add, ALU.max)\
                    .then_inc(carry_made, 1)
                dve.wait_ge(carry_ps, 1)
                seq.link(nc.vector.tensor_copy(carry[:, :], m.ps[:, 5, 0:2]))
                seq.did(scan(0, carry[:, 0:1]))
                seq.link(scan(1, carry[:, 1:2]))
                seq.link(nc.vector.tensor_tensor(best[0][:, :], best[0][:, :], best[1][:, :], ALU.max))
                nc.vector.tensor_tensor(chunk[:, :], chunk[:, :], best[0][:, :], ALU.subtract).then_inc(maxed, 1)


def weigh_edges(nc, m):
    WIDE = FEAT + HEADS
    with ExitStack() as ph:
        def sb(n, shape, dt=F32):
            return ph.enter_context(nc.sbuf_tensor(f"we_{n}", shape, dt))

        def sem(n):
            return ph.enter_context(nc.semaphore(f"we_{n}"))

        vj, msg, hot = sb("vj", [P, 2, GI, FEAT]), sb("msg", [P, 2, GI, WIDE]), sb("hot", [P, 2, GI, P])
        hot_made, weighed, msg_made, summed, added = (
            sem(n) for n in ("hot_made", "weighed", "msg_made", "summed", "added"))
        vj_in = [sem(f"vj_in{p}") for p in range(2)]
        GL = 4
        STEPS = NG // GL

        def exponentials(i, q):
            return m.ALPHA[:, bass.ds(i, 1), :, q * GI:(q + 1) * GI]

        def out_ps(half, j):
            return m.ps[:, 4 + 2 * half + j // 2, (j % 2) * WIDE:(j % 2 + 1) * WIDE]

        with nc.Block() as block:
            @block.sync
            def _(sp):
                with sp.Fori(0, NG // 2) as i:
                    for p in range(2):
                        sp.wait_ge(weighed, i * 2 + p + 1)
                        sp.dma_start(vj[:, p, :, :].rearrange("p j f -> p (j f)"),
                                     m.vj_spill[bass.ds(i * 2 + p, 1), :, :].rearrange("a p n -> (a p) n"))\
                            .then_inc(vj_in[p], 16)

            @block.gpsimd
            def _(pool):
                pool.sem_inc(weighed, 2)
                with pool.Fori(0, STEPS) as i:
                    for q in range(GL):
                        p = q % 2
                        pool.wait_ge(summed, i * 2 * GL + 2 * q + 2)
                        pool.wait_ge(vj_in[p], i * (GL // 2 * 16) + (q // 2 + 1) * 16)
                        nc.gpsimd.tensor_tensor(
                            msg[:, p, :, 0:FEAT].rearrange("p j (h c) -> p j h c", h=HEADS),
                            vj[:, p, :, :].rearrange("p j (h c) -> p j h c", h=HEADS),
                            exponentials(i, q).rearrange("p a h (j c) -> p j (a h) c", c=1)
                            .to_broadcast([P, GI, HEADS, CH]), ALU.mult).then_inc(weighed, 1)

            @block.scalar
            def _(act):
                with act.Fori(0, STEPS) as i:
                    for q in range(GL):
                        act.wait_ge(summed, i * 2 * GL + 2 * q + 2)
                        nc.scalar.activation(msg[:, q % 2, :, FEAT:WIDE],
                                             exponentials(i, q).rearrange("p a h j -> p j (a h)"), ACT.Copy)\
                            .then_inc(msg_made, 1)

            @block.vector
            def _(dve):
                nc.vector.memset(m.ACC[:, :, :], 0.0).then_inc(added, 8)
                with dve.Fori(0, NG // 2) as i:
                    for p in range(2):
                        blocks = loads(nc, dve, m.block_row, i * 2 * GI + p * GI, GI, NB - 1)
                        dve.wait_ge(summed, i * 4 + 2 * p + 2)
                        nc.vector.tensor_tensor(
                            hot[:, p, :, :],
                            m.iota_f[:, 0:P].rearrange("p (a w) -> p a w", a=1).to_broadcast([P, GI, P]),
                            m.rel[:, bass.ds(i * 2 * GI + p * GI, GI)].rearrange("p (t a) -> p t a", a=1)
                            .to_broadcast([P, GI, P]), ALU.is_equal).then_inc(hot_made, 1)
                        for half in range(2):
                            dve.wait_ge(summed, 4 + i * 4 + 2 * p + half + 1)
                            for j in range(4):
                                dve.wait_ge(added, 8 + i * 2 * GI + p * GI + half * 4 + j)
                                at = m.ACC[:, bass.ds(blocks[half * 4 + j], 1), :].rearrange("p a f -> p (a f)")
                                nc.vector.tensor_tensor(at, at, out_ps(half, j), ALU.add).then_inc(added, 1)

            @block.tensor
            def _(pe):
                pe.sem_inc(summed, 4)
                with pe.Fori(0, NG // 2) as i:
                    for p in range(2):
                        pe.wait_ge(hot_made, i * 2 + p + 1)
                        pe.wait_ge(weighed, i * 2 + p + 3)
                        pe.wait_ge(msg_made, i * 2 + p + 1)
                        for half in range(2):
                            pe.wait_ge(added, i * 2 * GI + p * GI + 4 * (half + 1))
                            for j in range(4):
                                last = nc.tensor.matmul(out_ps(half, j), hot[:, p, half * 4 + j, :],
                                                        msg[:, p, half * 4 + j, :], start=True, stop=True)
                            last.then_inc(summed, 1)


def finish_attention(nc, m):
    with ExitStack() as ph:
        def sb(n, shape, dt=F32):
            return ph.enter_context(nc.sbuf_tensor(f"fa_{n}", shape, dt))

        def sem(n):
            return ph.enter_context(nc.semaphore(f"fa_{n}"))

        rden = sb("rden", [P, NB, HEADS])
        seq_sem, product, act_taken, dve_taken = (sem(n) for n in ("dve_seq", "product", "act_taken", "dve_taken"))
        stages = ("skip", "turn", "mlp1", "mlp2", "back")
        on_act = ("turn", "mlp1", "mlp2")
        order = [(s, g) for s in stages for g in range(NGRP)]

        def count(n, act):
            return sum((order[k][0] in on_act) == act for k in range(n + 1))

        with nc.Block() as block:
            @block.tensor
            def _(pe):
                for n, (stage, g) in enumerate(order):
                    if n >= 2:
                        act = order[n - 2][0] in on_act
                        pe.wait_ge(act_taken if act else dve_taken, count(n - 2, act))
                    if stage != "skip":
                        act = order[n - NGRP][0] in on_act
                        pe.wait_ge(act_taken if act else dve_taken, count(n - NGRP, act))
                    for b in range(GB):
                        at = g * GB + b
                        cols = slice(at * P, (at + 1) * P)
                        bank = node_bank(m, n, b)
                        if stage == "skip":
                            nc.tensor.matmul(bank, m.HT[:, cols], m.W["Wskip"][:, :], start=True, stop=False)
                            last = nc.tensor.matmul(bank, m.ones[0:1, :], m.brow["bskip"][0:1, :],
                                                    start=False, stop=True)
                        elif stage == "turn":
                            last = nc.tensor.transpose(bank, m.D[:, at, :], m.ident[:, :])
                        elif stage == "mlp1":
                            last = nc.tensor.matmul(bank, m.W["M1"][:, :], m.AGGT[:, cols], start=True, stop=True)
                        elif stage == "mlp2":
                            last = nc.tensor.matmul(bank, m.W["M2"][:, :], m.HT[:, cols], start=True, stop=True)
                        else:
                            last = nc.tensor.transpose(bank, m.AGGT[:, cols], m.ident[:, :])
                    last.then_inc(product, 1)

            @block.scalar
            def _(act):
                for n, (stage, g) in enumerate(order):
                    if stage not in on_act:
                        continue
                    act.wait_ge(product, n + 1)
                    out = (m.HT if stage == "mlp1" else m.AGGT)[:, group_cols(g)]\
                        .rearrange("p (b f) -> p b f", b=GB)
                    if stage == "turn":
                        act.activation(out, node_group(m, n), ACT.Copy).then_inc(act_taken, 1)
                    else:
                        bias = m.b1col if stage == "mlp1" else m.b2col
                        act.activation(out, node_group(m, n), ACT.Gelu_apprx_tanh, bias=bias[:, 0:1])\
                           .then_inc(act_taken, 1)

            @block.vector
            def _(dve):
                seq = Sequence(dve, seq_sem)
                seq.link(nc.vector.tensor_scalar_add(rden[:, :, :], m.ACC[:, :, FEAT:FEAT + HEADS], 1e-16))
                seq.link(nc.vector.reciprocal(rden[:, :, :], rden[:, :, :]))
                for h in range(HEADS):
                    seq.did(nc.vector.tensor_tensor(m.D[:, :, h * CH:(h + 1) * CH], m.ACC[:, :, h * CH:(h + 1) * CH],
                                                    rden[:, :, h:h + 1].to_broadcast([P, NB, CH]), ALU.mult))
                seq.wait()
                done = 0
                for n, (stage, g) in enumerate(order):
                    if stage in on_act:
                        continue
                    dve.wait_ge(product, n + 1)
                    blocks = group_blocks(g)
                    if stage == "skip":
                        nc.vector.tensor_tensor(m.D[:, blocks, :], m.D[:, blocks, :], node_group(m, n), ALU.add)\
                            .then_inc(dve_taken, 1)
                        done += 1
                        dve.wait_ge(dve_taken, done)
                        seq.did(nc.vector.tensor_tensor(m.X[:, blocks, :], m.X[:, blocks, :], m.D[:, blocks, :],
                                                        ALU.add))
                    else:
                        if g == 0:
                            seq.wait()
                        nc.vector.tensor_tensor(m.X[:, blocks, :], m.X[:, blocks, :], node_group(m, n), ALU.add)\
                            .then_inc(dve_taken, 1)


def store_output(nc, m, out):
    with ExitStack() as ph:
        stored = ph.enter_context(nc.semaphore("stored"))
        with nc.Block() as block:
            @block.sync
            def _(sp):
                sp.dma_start(out[0:FULL * P, :].rearrange("(b p) f -> p b f", p=P), m.X[:, 0:FULL, :])\
                    .then_inc(stored, 16)
                sp.dma_start(out[FULL * P:NODES, :], m.X[0:LAST, FULL, :]).then_inc(stored, 16)
                sp.wait_ge(stored, 32)


def build(nc, t, out):
    with ExitStack() as ctx:
        def sb(name, shape, dt=F32):
            return ctx.enter_context(nc.sbuf_tensor(name, shape, dt))

        def dram(name, shape):
            return nc.dram_tensor(name, shape, F32, kind="Internal").ap()

        m = Memory()
        m.h_table = dram("h_table", [NB * P, FEAT])
        m.kv_table = dram("kv_table", [NB * P, 2 * FEAT])
        m.vj_spill = dram("vj_spill", [NG, P, GI * FEAT])
        m.alpha_dram = dram("alpha_dram", [HEADS, NI * P])
        m.ex_dram = dram("ex_dram", [HEADS, NI * P])
        m.marks_dram = dram("marks_dram", [3, NI * P])
        m.ea_tiles = t["ea_tiles"]
        m.X = sb("X", [P, NB, FEAT])
        m.H = sb("H", [P, NB, FEAT])
        m.D = sb("D", [P, NB, FEAT])
        m.HT = sb("HT", [P, NB * P])
        m.AGGT = sb("AGGT", [P, NB * P])
        m.rel = sb("rel", [P, NI])
        m.idx = sb("idx", [P, NI], I32)
        m.block_row = sb("block_row", [1, NI], I32)
        m.tile_row = sb("tile_row", [1, NI], I32)
        m.iota_i = sb("iota_i", [P, NI], I32)
        m.iota_f = sb("iota_f", [P, NI])
        m.pid_i = sb("pid_i", [P, KB + 1], I32)
        m.pid_f = sb("pid_f", [P, KB + 1])
        m.item_i = sb("item_i", [P, IKB], I32)
        m.ident = sb("ident", [P, P])
        m.ident16 = sb("ident16", [P, P], BF16)
        m.ones = sb("ones", [P, P])
        m.eps = sb("eps", [P, 1])
        m.rstd = sb("rstd", [P, NB])
        m.deg_in = sb("deg_in", [P, NB])
        m.deg_out = sb("deg_out", [P, NB])
        m.rcnt = sb("rcnt", [P, NB])
        m.isq_in = sb("isq_in", [P, NB])
        m.isq_out = sb("isq_out", [P, NB])
        m.W = {n: sb("w_" + n, [P, FEAT]) for n in ("W0a", "W0b", "W1", "Wq", "Wk", "Wv", "Wskip", "M1", "M2", "W3a", "W3b")}
        m.We = sb("w_We", [EDIM, FEAT])
        m.brow = {n: sb("r_" + n, [1, FEAT]) for n in ("b0", "bq", "bk", "bv", "bskip", "b3")}
        m.b1col = sb("b1col", [P, 1])
        m.b2col = sb("b2col", [P, 1])
        m.gamma = sb("gamma", [P, FEAT])
        m.beta = sb("beta", [P, FEAT])

        def psum(ph, name, shape, dt=F32):
            return ph.enter_context(nc.psum_tensor(name, shape, dt))

        with ExitStack() as ph:
            m.ps = psum(ph, "ps", [P, 8, 512])
            load_inputs(nc, m, t)
            list_items(nc, m, t)
            count_degrees(nc, m, t)

            normalise(nc, m, "n0")
            sum_neighbours(nc, m, "s0")
            project_pair(nc, m, "p0", m.W["W0a"], m.W["W0b"], m.brow["b0"], m.rcnt)

            normalise(nc, m, "n1")
            sum_neighbours(nc, m, "s1")
            project_sum(nc, m)

            normalise(nc, m, "n2")
        with ExitStack() as att:
            m.ALPHA = att.enter_context(nc.sbuf_tensor("ALPHA", [P, IB, HEADS, 32], F32))
            with ExitStack() as scoring:
                Q3 = scoring.enter_context(nc.sbuf_tensor("Q3", [P, NB, 3, FEAT], BF16))
                with ExitStack() as ph:
                    m.ps = psum(ph, "ps_qkv", [P, 8, 512])
                    project_qkv(nc, m, Q3)
                with ExitStack() as ph:
                    m.ps16 = psum(ph, "ps_hotT", [P, 2, 1024], BF16)
                    m.ps = psum(ph, "ps_terms", [P, 6, 512])
                    score_edges(nc, m, Q3)
            with ExitStack() as ph:
                m.ps = psum(ph, "ps_late", [P, 8, 512])
                softmax_edges(nc, m)
                m.ACC = att.enter_context(nc.sbuf_tensor("ACC", [P, NB, FEAT + HEADS], F32))
                weigh_edges(nc, m)
                finish_attention(nc, m)
        with ExitStack() as ph:
            m.ps = psum(ph, "ps_end", [P, 8, 512])
            normalise(nc, m, "n3", again=True)
            sum_neighbours(nc, m, "s3")
            project_pair(nc, m, "p3", m.W["W3a"], m.W["W3b"], m.brow["b3"], m.isq_in)
            store_output(nc, m, out)



def lay_out(a):
    src, dst, attr = a["src"], a["dst"], a["edge_attr_32"]

    def tiled(v, pad, tiles):
        return np.concatenate([v, np.full(tiles * P - len(v), pad, v.dtype)]).reshape(tiles, P)

    edge = np.zeros(1, dst.dtype) - 1
    attr = np.concatenate([attr, np.zeros((TILES * P - EDGES, EDIM), attr.dtype)])
    w0, w3 = a["L0_gnn_W_out"].T, a["L3_gnn_W"].T
    out = {
        "x": a["x"],
        "src_rows": tiled(src, 0, KB * P), "dst_rows": tiled(dst, PAD_DST, KB * P),
        "prev_rows": tiled(np.concatenate([edge, dst[:-1]]), PAD_DST, KB * P),
        "next_rows": tiled(np.concatenate([dst[1:], edge]), PAD_DST, KB * P),
        "first_dst": dst[::P], "last_dst": np.concatenate([dst[P - 1::P], dst[-1:]])[:TILES],
        "src_cols": tiled(src, PAD_DST, TILES).T, "dst_cols": tiled(dst, PAD_DST, TILES).T,
        "ea_tiles": attr.reshape(TILES, P, EDIM).transpose(0, 2, 1),
        "W0a": w0[:FEAT], "W0b": w0[FEAT:], "b0": a["L0_gnn_b_out"], "W1": a["L1_gnn_W"],
        "Wq": a["L2_gnn_Wq"], "bq": a["L2_gnn_bq"], "Wk": a["L2_gnn_Wk"], "bk": a["L2_gnn_bk"],
        "Wv": a["L2_gnn_Wv"], "bv": a["L2_gnn_bv"], "We": a["L2_gnn_We"],
        "Wskip": a["L2_gnn_Wskip"], "bskip": a["L2_gnn_bskip"],
        "M1": a["L2_gnn_W1"], "b1": a["L2_gnn_b1"], "M2": a["L2_gnn_W2"], "b2": a["L2_gnn_b2"],
        "gamma": a["L3_gnn_ln_gamma"], "beta": a["L3_gnn_ln_beta"],
        "W3a": w3[:FEAT], "W3b": w3[FEAT:], "b3": a["L3_gnn_b"],
    }
    return {n: np.ascontiguousarray(v) for n, v in out.items()}


def kernel(**inputs):
    import concourse.bacc as bacc
    from concourse.bass_utils import run_bass_kernel_spmd

    nc = bacc.Bacc("TRN2", target_bir_lowering=False, num_devices=1)
    arrays, tensors = {}, {}
    for name, a in lay_out({n: np.asarray(v) for n, v in inputs.items()}).items():
        arrays["in_" + name] = a
        tensors[name] = nc.dram_tensor("in_" + name, a.shape, mybir.dt.from_np(a.dtype), kind="ExternalInput").ap()
    out = nc.dram_tensor("out", [NODES, FEAT], F32, kind="ExternalOutput").ap()
    build(nc, tensors, out)
    return run_bass_kernel_spmd(nc, [arrays], core_ids=[0]).results[0]["out"]
```

```python
from contextlib import ExitStack

import numpy as np

import concourse.bass as bass
from concourse import mybir

F32 = mybir.dt.float32
BF16 = mybir.dt.bfloat16
I32 = mybir.dt.int32
ALU = mybir.AluOpType
ACT = mybir.ActivationFunctionType
AX = mybir.AxisListType.X

P = 128
NODES, FEAT = 3125, 128
EDGES, EDIM = 103125, 32
HEADS, CH = 4, 32
NB = -(-NODES // P)
FULL, LAST = NODES // P, NODES % P
TILES = -(-EDGES // P)
KB = -(-TILES // P)
GI = 8
NI = -(-(TILES + NB - 1) // 32) * 32
NG = NI // GI
IB = NI // 32
HALF = NI // 2
IKB = -(-NI // P)
CHUNKS = P // HEADS
CHUNK = NI * P // CHUNKS
PAIRS = -(-TILES // 2)
PKB = -(-PAIRS // P)
DG = 8
NDG = -(-NODES // DG)
DGW = DG * NB
NA = -(-(PAIRS + NDG - 1) // 16) * 16
CHK = 8
CW = -(-NDG * DG // (CHK * 4)) * 4
COLS = CHK * CW
EXACT = 256
BIG = 1.0e37
EPS = 1e-5
PAD_DST = 8191
NGRP = 5
GB = NB // NGRP
assert GB * NGRP == NB and HALF <= 512 and DGW <= 256 and NA // 2 <= 512
IN_RANGE = "the value is a node block or edge tile number that the chip clamped to its table"


class Memory:
    pass


def new_semaphore(nc, m, name):
    m.semaphores.append(nc.alloc_semaphore(name))
    return m.semaphores[-1]


def clear_semaphores(nc, m):
    nc.clear_and_free_semaphores(m.semaphores)
    nc.all_engine_barrier()
    m.semaphores = []


class Sequence:

    def __init__(self, engine, sem):
        self.engine, self.sem, self.n, self.static = engine, sem, 0, 0

    def did(self, instruction):
        instruction.then_inc(self.sem, 1)
        self.n = self.n + 1
        self.static += 1

    def wait(self):
        self.engine.wait_ge(self.sem, self.n)

    def link(self, instruction):
        self.did(instruction)
        self.wait()

    def enter(self, i, per_step):
        self.start, self.per_step, self.before = self.n, per_step, self.static
        self.n = self.start + i * per_step

    def leave(self, steps):
        assert self.static - self.before == self.per_step, self.static - self.before
        self.n = self.start + steps * self.per_step


def loads(nc, engine, row, first, count, top):
    _, values = nc.values_load_multi_w_load_instructions(
        row[0:1, bass.ds(first, count)], engines=[engine.engine], min_val=0, max_val=top,
        skip_runtime_bounds_check_because=IN_RANGE)
    return values


def node_bank(m, n, block):
    return m.ps[:, 2 * (n % 2) + block // 4, (block % 4) * P:(block % 4 + 1) * P]


def node_group(m, n):
    flat = m.ps[:, 2 * (n % 2):2 * (n % 2) + 2, :].rearrange("p k n -> p (k n)")
    return flat[:, 0:GB * FEAT].rearrange("p (b f) -> p b f", b=GB)


def group_blocks(g):
    return slice(g * GB, (g + 1) * GB)


def group_cols(g):
    return slice(g * GB * P, (g + 1) * GB * P)



def make_constants(nc, m):
    with ExitStack() as ph:
        counted = new_semaphore(nc, m, ("counted"))
        iota_i = ph.enter_context(nc.sbuf_tensor("iota_i", [P, NI], I32))
        pid_i = ph.enter_context(nc.sbuf_tensor("pid_i", [P, KB], I32))
        with nc.Block() as block:
            @block.gpsimd
            def _(pool):
                pool.iota(iota_i[:, :], [[1, NI]], base=0, channel_multiplier=0).then_inc(counted, 1)
                pool.iota(pid_i[:, :], [[P, KB]], base=0, channel_multiplier=1).then_inc(counted, 1)

            @block.vector
            def _(dve):
                nc.vector.memset(m.ones[:, :], 1.0)
                nc.vector.memset(m.eps[:, :], EPS)
                nc.vector.memset(m.rel[:, NI:], -1.0)
                nc.vector.memset(m.tile_row[:, NI:], 0)
                dve.wait_ge(counted, 2)
                nc.vector.tensor_copy(m.iota_f[:, :], iota_i[:, :])
                nc.vector.tensor_copy(m.pid_f[:, :], pid_i[:, :])


def load_inputs(nc, m, t):
    with ExitStack() as ph:
        def sem(name):
            return new_semaphore(nc, m, (name))

        nodes_in, weights_in, cleared, identity = (sem(n) for n in ("nodes_in", "weights_in", "cleared", "identity"))
        with nc.Block() as block:
            @block.vector
            def _(dve):
                nc.vector.memset(m.X[:, FULL, :], 0.0).then_inc(cleared, 1)
                nc.vector.memset(m.AGGT[:, COLS:], 0.0)
                nc.vector.memset(m.degT[:, COLS:], 0.0)
                nc.vector.memset(m.ones16[:, :], 1.0)
                dve.wait_ge(identity, 2)
                nc.vector.tensor_copy(m.ident16[:, :], m.ident[:, :])

            @block.gpsimd
            def _(pool):
                pool.memset(m.ident[:, :], 0.0).then_inc(identity, 1)
                pool.wait_ge(identity, 1)
                pool.affine_select(out=m.ident[:, :], in_=m.ident[:, :], compare_op=ALU.not_equal, fill=1.0,
                                   base=0, pattern=[[-1, P]], channel_multiplier=1).then_inc(identity, 1)

            @block.sync
            def _(sp):
                sp.wait_ge(cleared, 1)
                sp.dma_start(m.X[:, 0:FULL, :],
                             t["x"][0:FULL * P, :].rearrange("(b p) f -> p b f", p=P)).then_inc(nodes_in, 16)
                sp.dma_start(m.X[0:LAST, FULL, :], t["x"][FULL * P:NODES, :]).then_inc(nodes_in, 16)
                sp.wait_ge(nodes_in, 32)

            @block.scalar
            def _(act):
                n = 0
                for name, tile in m.W.items():
                    act.dma_start(tile[:, :], t[name]).then_inc(weights_in, 16)
                    n += 16
                act.dma_start(m.We[:, :], t["We"]).then_inc(weights_in, 16)
                for name, tile in m.brow.items():
                    act.dma_start(tile[0:1, :], t[name].rearrange("(a f) -> a f", a=1)).then_inc(weights_in, 16)
                    n += 16
                for name, tile in (("b1", m.b1col), ("b2", m.b2col)):
                    act.dma_start(tile[:, :], t[name].rearrange("(f a) -> f a", a=1)).then_inc(weights_in, 16)
                for name, tile in (("gamma", m.gamma), ("beta", m.beta)):
                    act.dma_start(tile[:, :], t[name].rearrange("(a f) -> a f", a=1).to_broadcast([P, FEAT]))\
                       .then_inc(weights_in, 16)
                act.wait_ge(weights_in, n + 16 * 5)



def staircase_memory(nc, m, ph, name, units, kb, items, shift):
    def sb(n, shape, dt=F32):
        return ph.enter_context(nc.sbuf_tensor(f"{name}_{n}", shape, dt))

    s = Memory()
    s.units, s.kb, s.items, s.shift = units, kb, items, shift
    s.sel = sb("sel", [P, kb, items])
    s.ends_i = sb("ends_i", [1, 2, units], I32)
    s.group0, s.length = sb("group0", [1, units]), sb("length", [1, units])
    s.row = sb("row", [1, 3, kb * P])
    s.cols = sb("cols", [P, 3, kb])
    s.shift_b = sb("shift_b", [P, kb, P])
    s.row_made, s.cols_ps, s.cols_made = (
        new_semaphore(nc, m, (f"{name}_{n}")) for n in ("row_made", "cols_ps", "cols_made"))
    return s


def find_items(nc, m, dve, seq, s):
    seq.did(nc.vector.memset(s.row[:, :, :], 0.0))
    seq.link(nc.vector.tensor_single_scalar(s.ends_i[:, :, :], s.ends_i[:, :, :], s.shift, ALU.arith_shift_right))
    seq.did(nc.vector.tensor_copy(s.group0[:, :], s.ends_i[0:1, 0, :]))
    seq.link(nc.vector.tensor_copy(s.length[:, :], s.ends_i[0:1, 1, :]))
    seq.link(nc.vector.tensor_tensor(s.length[:, :], s.length[:, :], s.group0[:, :], ALU.subtract))
    seq.link(nc.vector.tensor_scalar_add(s.length[:, :], s.length[:, :], 1.0))
    start, end, shift = (s.row[0:1, k, 0:s.units] for k in range(3))
    seq.link(nc.vector.tensor_tensor_scan(end, s.length[:, :], s.length[:, :], 0.0, ALU.add, ALU.max))
    seq.link(nc.vector.tensor_tensor(start, end, s.length[:, :], ALU.subtract))
    nc.vector.tensor_tensor(shift, s.group0[:, :], start, ALU.subtract).then_inc(s.row_made, 1)
    dve.wait_ge(s.cols_ps, 1)
    nc.vector.tensor_copy(s.cols[:, :, :], m.ps[:, 7, 0:3 * s.kb].rearrange("p (a k) -> p a k", a=3))\
        .then_inc(s.cols_made, 1)
    dve.wait_ge(s.cols_made, 1)
    iota = m.iota_f[:, 0:s.items]
    for k in range(s.kb):
        seq.did(nc.vector.tensor_copy(s.shift_b[:, k, :], s.cols[:, 2, k:k + 1].to_broadcast([P, P])))
        seq.link(nc.vector.tensor_scalar(s.sel[:, k, :], iota, s.cols[:, 0, k:k + 1], None, ALU.is_ge))
        seq.link(nc.vector.scalar_tensor_tensor(s.sel[:, k, :], iota, s.cols[:, 1, k:k + 1], s.sel[:, k, :],
                                                ALU.is_lt, ALU.mult))


def turn_item_rows(nc, m, pe, s):
    pe.wait_ge(s.row_made, 1)
    for a in range(3):
        for k in range(s.kb):
            last = nc.tensor.matmul(m.ps[:, 7, a * s.kb + k:a * s.kb + k + 1],
                                    s.row[0:1, a, k * P:(k + 1) * P], m.ones[0:1, 0:1], start=True, stop=True)
    last.then_inc(s.cols_ps, 1)


def list_items(nc, m, t):
    with ExitStack() as ph:
        def sb(name, shape, dt=F32):
            return ph.enter_context(nc.sbuf_tensor(name, shape, dt))

        def sem(name):
            return new_semaphore(nc, m, (name))

        s = staircase_memory(nc, m, ph, "items", TILES, KB, NI, 7)
        raw = [sb(f"raw_{n}", [P, KB, P], I32) for n in ("src", "dst", "prev", "next")]
        src_f, dst_f, first_f, last_f = (sb(n, [P, KB, P]) for n in ("src_f", "dst_f", "first_f", "last_f"))
        block_f = sb("block_f", [P, NI])
        marks = sb("marks", [P, 3, IKB, P])
        block_c = sb("block_c", [P, IKB])

        tiles_in, ends_in, sel_made, rows_made, expanded, taken, marked, kept = (
            sem(n) for n in ("tiles_in", "ends_in", "sel_made", "rows_made",
                             "expanded", "expanded_taken", "marked", "marks_kept"))
        dve_seq = sem("list_dve_seq")
        jobs = [(what, h) for what in ("block", "tile", "src", "dst") for h in range(2)]
        jobs += [(what, k) for k in range(IKB) for what in ("block_c", "first", "last", "dst_c")]

        with nc.Block() as block:
            @block.sync
            def _(sp):
                for k, name in enumerate(("first_dst", "last_dst")):
                    sp.dma_start(s.ends_i[0:1, k, :], t[name].rearrange("(a n) -> a n", a=1)).then_inc(ends_in, 16)
                for k, name in enumerate(("src_rows", "dst_rows", "prev_rows", "next_rows")):
                    sp.dma_start(raw[k][:, :, :], t[name].rearrange("(k p) e -> p k e", p=P)).then_inc(tiles_in, 16)
                sp.wait_ge(marked, 1)
                full = NI // P
                for k in range(3):
                    view = m.marks_dram[k]
                    sp.dma_start(view[0:full * P * P].rearrange("(b p e) -> p b e", p=P, e=P),
                                 marks[:, k, 0:full, :]).then_inc(kept, 16)
                    sp.dma_start(view[full * P * P:NI * P].rearrange("(p e) -> p e", e=P),
                                 marks[0:NI % P, k, full, :]).then_inc(kept, 16)
                sp.wait_ge(kept, 16 * 6)

            @block.vector
            def _(dve):
                seq = Sequence(dve, dve_seq)
                dve.wait_ge(ends_in, 32)
                find_items(nc, m, dve, seq, s)
                nc.vector.memset(marks[:, :, :, :], 0.0).then_inc(sel_made, 1)
                dve.wait_ge(tiles_in, 64)
                seq.did(nc.vector.tensor_copy(src_f[:, :, :], raw[0][:, :, :]))
                seq.did(nc.vector.tensor_copy(dst_f[:, :, :], raw[1][:, :, :]))
                seq.did(nc.vector.tensor_tensor(first_f[:, :, :], raw[1][:, :, :], raw[2][:, :, :], ALU.not_equal))
                nc.vector.tensor_tensor(last_f[:, :, :], raw[1][:, :, :], raw[3][:, :, :], ALU.not_equal)\
                    .then_inc(rows_made, 1)
                seq.wait()
                for n, (what, k) in enumerate(jobs):
                    dve.wait_ge(expanded, n + 1)
                    half = slice(k * HALF, (k + 1) * HALF)
                    got = m.ps[:, n % 4, 0:HALF]
                    rows = min(P, NI - k * P) if k < IKB else P
                    if what == "block":
                        seq.link(nc.vector.tensor_tensor(block_f[:, half], got, m.iota_f[:, half], ALU.add))
                        seq.link(nc.vector.tensor_scalar_min(block_f[:, half], block_f[:, half], float(NB - 1)))
                        last = nc.vector.tensor_copy(m.block_row[0:1, half], block_f[0:1, half])
                    elif what == "tile":
                        last = nc.vector.tensor_copy(m.tile_row[0:1, half], got[0:1, :])
                    elif what == "src":
                        last = nc.vector.tensor_copy(m.idx[:, half], got)
                    elif what == "dst":
                        last = nc.vector.scalar_tensor_tensor(m.rel[:, half], block_f[:, half], -float(P), got,
                                                              ALU.mult, ALU.add)
                    elif what == "block_c":
                        c = slice(k, k + 1)
                        seq.link(nc.vector.tensor_tensor(block_c[0:rows, c], m.ps[0:rows, n % 4, 0:1],
                                                         m.pid_f[0:rows, c], ALU.add))
                        seq.link(nc.vector.tensor_scalar_min(block_c[0:rows, c], block_c[0:rows, c],
                                                             float(NB - 1)))
                        last = nc.vector.tensor_scalar(block_c[0:rows, c], block_c[0:rows, c], float(P), None,
                                                       ALU.mult)
                    elif what == "dst_c":
                        z = marks[0:rows, 2, k, :]
                        seq.link(nc.vector.tensor_scalar(z, m.ps[0:rows, n % 4, 0:P], block_c[0:rows, k:k + 1],
                                                         63.5, ALU.subtract, ALU.subtract))
                        seq.link(nc.vector.tensor_tensor(z, z, z, ALU.mult))
                        last = nc.vector.tensor_scalar(z, z, 64.0 * 64.0, -BIG, ALU.is_gt, ALU.mult)
                    else:
                        last = nc.vector.tensor_scalar(marks[0:rows, ("first", "last").index(what), k, :],
                                                       m.ps[0:rows, n % 4, 0:P], -BIG, None, ALU.mult)
                    last.then_inc(taken, 1)
                    dve.wait_ge(taken, n + 1)
                nc.vector.tensor_copy(block_c[:, 0:1], m.iota_f[:, 0:1]).then_inc(marked, 1)

            @block.tensor
            def _(pe):
                turn_item_rows(nc, m, pe, s)
                pe.wait_ge(sel_made, 1)
                pe.wait_ge(rows_made, 1)
                for n, (what, k) in enumerate(jobs):
                    if n >= 4:
                        pe.wait_ge(taken, n - 3)
                    for kk in range(KB):
                        edge = dict(start=kk == 0, stop=kk == KB - 1)
                        if what in ("block", "tile", "src", "dst"):
                            rhs = s.sel[:, kk, k * HALF:(k + 1) * HALF]
                            if what == "tile":
                                last = nc.tensor.matmul(m.ps[0:1, n % 4, 0:HALF], m.pid_f[:, kk:kk + 1], rhs, **edge)
                            else:
                                lhsT = dict(block=s.shift_b, src=src_f, dst=dst_f)[what][:, kk, :]
                                last = nc.tensor.matmul(m.ps[:, n % 4, 0:HALF], lhsT, rhs, **edge)
                        else:
                            rows = min(P, NI - k * P)
                            lhsT = s.sel[:, kk, k * P:k * P + rows]
                            rhs = dict(block_c=s.cols[:, 2, kk:kk + 1], first=first_f[:, kk, :],
                                       last=last_f[:, kk, :], dst_c=dst_f[:, kk, :])[what]
                            width = 1 if what == "block_c" else P
                            last = nc.tensor.matmul(m.ps[0:rows, n % 4, 0:width], lhsT, rhs, **edge)
                    last.then_inc(expanded, 1)



def list_adjacency_items(nc, m, t):
    HA = NA // 2
    with ExitStack() as ph:
        def sb(name, shape, dt=F32):
            return ph.enter_context(nc.sbuf_tensor(name, shape, dt))

        def sem(name):
            return new_semaphore(nc, m, (name))

        s = staircase_memory(nc, m, ph, "aitems", PAIRS, PKB, NA, DG.bit_length() - 1)
        raw = [sb(f"araw_{n}", [P, PKB, 2, P], I32) for n in ("src", "dst")]
        low_i, high_i = sb("low_i", [P, PKB, 2, P], I32), sb("high_i", [P, PKB, 2, P], I32)
        low_f, high_f, key_f = (sb(n, [P, PKB, 2, P]) for n in ("alow_f", "ahigh_f", "akey_f"))
        group_f = sb("group_f", [P, NA])
        pairs_in, ends_in, ready, expanded, taken, dve_seq = (
            sem(n) for n in ("pairs_in", "aends_in", "aready", "aexpanded", "ataken", "alist_dve_seq"))
        jobs = [("group", 0, h) for h in range(2)] + [(w, e, h) for w in ("key", "low") for e in range(2)
                                                      for h in range(2)]
        with nc.Block() as block:
            @block.sync
            def _(sp):
                for k, name in enumerate(("first_dst2", "last_dst2")):
                    sp.dma_start(s.ends_i[0:1, k, :], t[name].rearrange("(a n) -> a n", a=1)).then_inc(ends_in, 16)
                for k, name in enumerate(("src_pairs", "dst_pairs")):
                    sp.dma_start(raw[k][:, :, :, :], t[name].rearrange("(k p) (h e) -> p k h e", p=P, h=2))\
                        .then_inc(pairs_in, 16)

            @block.vector
            def _(dve):
                seq = Sequence(dve, dve_seq)
                dve.wait_ge(ends_in, 32)
                find_items(nc, m, dve, seq, s)
                seq.did(nc.vector.memset(m.key[:, :, NA:], -1.0))
                seq.did(nc.vector.memset(m.low[:, :, NA:], 0.0))
                dve.wait_ge(pairs_in, 32)
                seq.did(nc.vector.tensor_single_scalar(low_i[:, :, :, :], raw[0][:, :, :, :], P - 1, ALU.bitwise_and))
                seq.did(nc.vector.tensor_single_scalar(high_i[:, :, :, :], raw[0][:, :, :, :], 7,
                                                       ALU.arith_shift_right))
                seq.link(nc.vector.tensor_copy(key_f[:, :, :, :], raw[1][:, :, :, :]))
                seq.did(nc.vector.tensor_copy(low_f[:, :, :, :], low_i[:, :, :, :]))
                seq.link(nc.vector.tensor_copy(high_f[:, :, :, :], high_i[:, :, :, :]))
                nc.vector.scalar_tensor_tensor(key_f[:, :, :, :], key_f[:, :, :, :], float(NB), high_f[:, :, :, :],
                                               ALU.mult, ALU.add).then_inc(ready, 1)
                for n, (what, e, h) in enumerate(jobs):
                    dve.wait_ge(expanded, n + 1)
                    half = slice(h * HA, (h + 1) * HA)
                    got = m.ps[:, n % 4, 0:HA]
                    if what == "group":
                        seq.link(nc.vector.tensor_tensor(group_f[:, half], got, m.iota_f[:, half], ALU.add))
                        seq.link(nc.vector.tensor_scalar_min(group_f[:, half], group_f[:, half], float(NDG - 1)))
                        last = nc.vector.tensor_copy(m.group_row[0:1, half], group_f[0:1, half])
                    elif what == "key":
                        last = nc.vector.scalar_tensor_tensor(m.key[:, e, half], group_f[:, half], -float(DGW), got,
                                                              ALU.mult, ALU.add)
                    else:
                        last = nc.vector.tensor_scalar(m.low[:, e, half], got, (1.0, -1.0)[e], None, ALU.mult)
                    last.then_inc(taken, 1)

            @block.tensor
            def _(pe):
                turn_item_rows(nc, m, pe, s)
                pe.wait_ge(ready, 1)
                for n, (what, e, h) in enumerate(jobs):
                    if n >= 4:
                        pe.wait_ge(taken, n - 3)
                    for kk in range(PKB):
                        lhsT = s.shift_b[:, kk, :] if what == "group" else dict(key=key_f, low=low_f)[what][:, kk, e, :]
                        last = nc.tensor.matmul(m.ps[:, n % 4, 0:HA], lhsT, s.sel[:, kk, h * HA:(h + 1) * HA],
                                                start=kk == 0, stop=kk == PKB - 1)
                    last.then_inc(expanded, 1)


def build_adjacency(nc, m):
    G, Q = 8, 4
    with ExitStack() as ph:
        def sb(name, shape, dt=F32):
            return ph.enter_context(nc.sbuf_tensor(name, shape, dt))

        def sem(name):
            return new_semaphore(nc, m, (name))

        A = sb("A", [P, NB, COLS], BF16)
        iota_wide = sb("iota_wide", [P, DGW, Q], BF16)
        hot_key, hot_low = sb("hot_key", [P, 2, 2, 2, DGW, Q], BF16), sb("hot_low", [P, 2, 2, P, Q], BF16)
        hot_low_act, low_now = sb("hot_low_act", [P, 2, G, P], BF16), sb("low_now", [P, G])
        iota_made, hot_made, low_made, low_staged, apart, placed, added, cleared, kept = (
            new_semaphore(nc, m, n) for n in ("iota_made", "ahot_made", "alow_made", "low_staged", "apart",
                                              "placed", "aadded", "acleared", "akept"))
        START = 4
        STEPS = NA // (2 * G)

        def piece(half, j):
            return m.ps[:, 4 + 2 * half + j // 2, (j % 2) * 256:(j % 2) * 256 + DGW]

        def one_hot_low(first, p):
            keys = m.low[:, 0:1, bass.ds(first, G)].rearrange("p (w a) (h q) -> p h (a w) q", w=1, h=2)
            return nc.vector.tensor_tensor(
                hot_low[:, p, :, :, :],
                iota_wide[:, 0:P, :].rearrange("p (h w) q -> p h w q", h=1).to_broadcast([P, 2, P, Q]),
                keys.to_broadcast([P, 2, P, Q]), ALU.is_equal)

        def one_hot_keys(first, p, half, part):
            w = slice(part * 2 * NB, (part + 1) * 2 * NB)
            return nc.vector.tensor_tensor(
                hot_key[:, p, half, :, w, :],
                iota_wide[:, w, :].rearrange("p (e w) q -> p e w q", e=1).to_broadcast([P, 2, 2 * NB, Q]),
                m.key[:, :, bass.ds(first + half * Q, Q)].rearrange("p e (w q) -> p e w q", w=1)
                .to_broadcast([P, 2, 2 * NB, Q]), ALU.is_equal)

        with nc.Block() as block:
            @block.gpsimd
            def _(pool):
                nc.gpsimd.memset(A[:, NB // 2:NB, :].bitcast(F32), 0.0).then_inc(cleared, 1)

            @block.vector
            def _(dve):
                nc.vector.tensor_copy(iota_wide[:, :, :], m.iota_f[:, 0:DGW].rearrange("p (w q) -> p w q", q=1)
                                      .to_broadcast([P, DGW, Q])).then_inc(iota_made, 1)
                dve.wait_ge(iota_made, 1)
                one_hot_low(0, 0)
                for half in range(2):
                    for part in range(4):
                        last = one_hot_keys(0, 0, half, part)
                    last.then_inc(hot_made, 1)
                nc.vector.memset(A[:, 0:NB // 2, :].bitcast(F32), 0.0).then_inc(added, G)
                dve.wait_ge(cleared, 1)
                with dve.Fori(0, STEPS) as i:
                    for p in range(2):
                        first = i * (2 * G) + p * G
                        one_hot_low(first + G, 1 - p)
                        groups = loads(nc, dve, m.group_row, first, G, NDG - 1)
                        for half in range(2):
                            dve.wait_ge(placed, START + i * 4 + 2 * p + half + 1)
                            for j in range(G // 2):
                                jj = half * (G // 2) + j
                                dve.wait_ge(added, G + first + jj)
                                at = A[:, :, bass.ds(groups[jj] * DG, DG)]
                                nc.vector.tensor_tensor(at, at, piece(half, j).rearrange("p (d h) -> p h d", h=NB),
                                                        ALU.add).then_inc(added, 1)
                                last = one_hot_keys(first + G, 1 - p, half, j)
                            last.then_inc(hot_made, 1)

            @block.scalar
            def _(act):
                act.sem_inc(low_made, 1)
                with act.Fori(0, STEPS) as i:
                    for p in range(2):
                        act.wait_ge(placed, i * 4 + 2 * p + 2)
                        act.activation(low_now[:, :], m.low[:, 1, bass.ds(i * (2 * G) + p * G, G)], ACT.Copy)\
                            .then_inc(low_staged, 1)
                        act.wait_ge(low_staged, i * 2 + p + 1)
                        act.wait_ge(low_made, i * 2 + p + 1)
                        for j in range(G):
                            last = act.activation(hot_low_act[:, p, j, :], m.iota_f[:, 0:P], ACT.Abs,
                                                  bias=low_now[:, j:j + 1])
                        last.then_inc(apart, 1)
                        act.wait_ge(apart, i * 2 + p + 1)
                        act.activation(hot_low_act[:, p, :, :], hot_low_act[:, p, :, :], ACT.Relu, scale=-1.0,
                                       bias=m.ones[:, 0:1]).then_inc(low_made, 1)

            @block.tensor
            def _(pe):
                pe.sem_inc(placed, START)
                with pe.Fori(0, STEPS) as i:
                    for p in range(2):
                        pe.wait_ge(low_made, i * 2 + p + 2)
                        for half in range(2):
                            pe.wait_ge(hot_made, i * 4 + 2 * p + half + 1)
                            pe.wait_ge(added, i * (2 * G) + p * G + (G // 2) * (half + 1))
                            for j in range(G // 2):
                                jj = half * (G // 2) + j
                                for e in range(2):
                                    lows = hot_low_act[:, p, jj, :] if e else hot_low[:, p, half, :, j]
                                    last = nc.tensor.matmul(piece(half, j), lows, hot_key[:, p, half, e, :, j], start=e == 0, stop=e == 1)
                            last.then_inc(placed, 1)

            @block.sync
            def _(sp):
                sp.wait_ge(added, NA + G)
                for c in range(CHK):
                    sp.dma_start(m.adj_dram[c].rearrange("p (h d) -> p h d", h=NB), A[:, :, c * CW:(c + 1) * CW])\
                        .then_inc(kept, 16)
                sp.wait_ge(kept, 16 * CHK)


def apply_adjacency(nc, m, name, rows, degrees):
    with ExitStack() as ph:
        def sb(n, shape, dt=F32):
            return ph.enter_context(nc.sbuf_tensor(f"{name}_{n}", shape, dt))

        def sem(n):
            return new_semaphore(nc, m, (f"{name}_{n}"))

        parts = sb("parts", [P, 3, NB, FEAT], BF16)
        rest = sb("rest", [P, NB, FEAT])
        adj = sb("adj", [P, 2, NB, CW], BF16)
        per_chunk = sb("per_chunk", [P, NB, CHK])
        unused = sb("unused", [P, 4, CW], BF16)
        split, summed, taken, act_read, dve_seq = (sem(n) for n in ("split", "summed", "taken", "act_read", "dve_seq"))
        adj_in = [sem(f"adj_in{p}") for p in range(2)]
        per = 2 if degrees else 1
        with nc.Block() as block:
            @block.sync
            def _(sp):
                for c in range(CHK):
                    if c >= 2:
                        sp.wait_ge(summed, c - 1)
                        if degrees:
                            sp.wait_ge(act_read, NB * (c - 1))
                    sp.dma_start(adj[:, c % 2, :, :].rearrange("p h d -> p (h d)"), m.adj_dram[c])\
                        .then_inc(adj_in[c % 2], 16)

            @block.vector
            def _(dve):
                nc.vector.tensor_copy(parts[:, 0, :, :], rows[:, 0:NB, :]).then_inc(split, 1)
                dve.wait_ge(split, 1)
                seq = Sequence(dve, dve_seq)
                seq.link(nc.vector.tensor_tensor(rest[:, :, :], rows[:, 0:NB, :], parts[:, 0, :, :], ALU.subtract))
                nc.vector.tensor_copy(parts[:, 1, :, :], rest[:, :, :]).then_inc(split, 1)
                dve.wait_ge(split, 2)
                seq.link(nc.vector.tensor_tensor(rest[:, :, :], rest[:, :, :], parts[:, 1, :, :], ALU.subtract))
                nc.vector.tensor_copy(parts[:, 2, :, :], rest[:, :, :]).then_inc(split, 1)
                for c in range(CHK):
                    cols = slice(c * CW, (c + 1) * CW)
                    dve.wait_ge(summed, c + 1)
                    nc.vector.tensor_copy(m.AGGT[:, cols], m.ps[:, c % 2, 0:CW]).then_inc(taken, 1)
                    if degrees:
                        nc.vector.tensor_copy(m.degT[:, cols], m.ps[:, 2 + c % 2, 0:CW]).then_inc(taken, 1)
                if degrees:
                    dve.wait_ge(act_read, NB * CHK)
                    dve.wait_ge(taken, per * CHK)
                    seq.did(nc.vector.tensor_reduce(m.deg_out[:, :], per_chunk[:, :, :], AX, ALU.add))
                    seq.link(nc.vector.tensor_reduce(m.most[0:1, 0:1], m.degT[0:1, 0:COLS], AX, ALU.max))
                    seq.link(nc.vector.tensor_single_scalar(m.most[0:1, 0:1], m.most[0:1, 0:1], float(EXACT),
                                                            ALU.is_ge))
                    seq.link(nc.vector.tensor_copy(m.general[0:1, 0:1], m.most[0:1, 0:1]))

            @block.scalar
            def _(act):
                if not degrees:
                    return
                for c in range(CHK):
                    act.wait_ge(adj_in[c % 2], 16 * (c // 2 + 1))
                    for h in range(NB):
                        n = c * NB + h
                        if n >= 4:
                            act.wait_ge(act_read, n - 3)
                        act.activation(unused[:, n % 4, :], adj[:, c % 2, h, :], ACT.Copy,
                                       accum_out=per_chunk[:, h, c:c + 1]).then_inc(act_read, 1)

            @block.tensor
            def _(pe):
                for c in range(CHK):
                    pe.wait_ge(adj_in[c % 2], 16 * (c // 2 + 1))
                    if c >= 2:
                        pe.wait_ge(taken, per * (c - 1))
                    for k in range(3):
                        pe.wait_ge(split, k + 1)
                        for h in range(NB):
                            last = nc.tensor.matmul(m.ps[:, c % 2, 0:CW], parts[:, k, h, :], adj[:, c % 2, h, :],
                                                    start=k == 0 and h == 0, stop=k == 2 and h == NB - 1)
                    for h in range(NB if degrees else 0):
                        last = nc.tensor.matmul(m.ps[:, 2 + c % 2, 0:CW], m.ones16[:, :], adj[:, c % 2, h, :],
                                                start=h == 0, stop=h == NB - 1)
                    last.then_inc(summed, 1)



def when_general(m, engine):
    return engine.If(engine.value_load(m.general[0:1, 0:1], min_val=0, max_val=1) > 0)


def count_sources(nc, m, t):
    TG = 13
    STEPS = TILES // TG
    assert TG * STEPS == TILES
    with ExitStack() as ph:
        def sb(name, shape, dt=F32):
            return ph.enter_context(nc.sbuf_tensor(name, shape, dt))

        def sem(name):
            return new_semaphore(nc, m, (name))

        node_i, part_i = sb("node_i", [P, TILES], I32), sb("part_i", [P, TILES], I32)
        low, high = sb("low", [P, TILES]), sb("high", [P, TILES])
        hot_low, hot_high = sb("hot_l", [P, TG, P], BF16), sb("hot_h", [P, TG, NB], BF16)
        cols_in, seq_sem, hot, counted, added = (
            sem(n) for n in ("edge_cols_in", "deg_dve_seq", "hot_made", "counted_tiles", "degrees_added"))
        with nc.Block() as block:
            @block.sync
            def _(sp):
                with when_general(m, sp):
                    sp.dma_start(node_i[:, :], t["src_cols"]).then_inc(cols_in, 16)

            @block.vector
            def _(dve):
                seq = Sequence(dve, seq_sem)
                with when_general(m, dve):
                    seq.did(nc.vector.memset(m.deg_out[:, :], 0.0))
                    dve.wait_ge(cols_in, 16)
                    seq.link(nc.vector.tensor_single_scalar(part_i[:, :], node_i[:, :], P - 1, ALU.bitwise_and))
                    seq.link(nc.vector.tensor_copy(low[:, :], part_i[:, :]))
                    seq.link(nc.vector.tensor_single_scalar(part_i[:, :], node_i[:, :], 7, ALU.arith_shift_right))
                    seq.link(nc.vector.tensor_copy(high[:, :], part_i[:, :]))
                    with dve.Fori(0, STEPS) as i:
                        cols = bass.ds(i * TG, TG)
                        for out, width, part in ((hot_low, P, low), (hot_high, NB, high)):
                            nc.vector.tensor_tensor(
                                out[:, :, :],
                                m.iota_f[:, 0:width].rearrange("p (a w) -> p a w", a=1).to_broadcast([P, TG, width]),
                                part[:, cols].rearrange("p (t a) -> p t a", a=1).to_broadcast([P, TG, width]),
                                ALU.is_equal).then_inc(hot, 1)
                        dve.wait_ge(counted, i + 1)
                        nc.vector.tensor_tensor(m.deg_out[:, :], m.deg_out[:, :], m.ps[:, 0, 0:NB], ALU.add)\
                            .then_inc(added, 1)
                        dve.wait_ge(added, i + 1)

            @block.tensor
            def _(pe):
                with when_general(m, pe):
                    with pe.Fori(0, STEPS) as i:
                        pe.wait_ge(hot, i * 2 + 2)
                        for j in range(TG):
                            last = nc.tensor.matmul(m.ps[:, 0, 0:NB], hot_low[:, j, :], hot_high[:, j, :],
                                                    start=j == 0, stop=j == TG - 1)
                        last.then_inc(counted, 1)


def scale_degrees(nc, m):
    with ExitStack() as ph:
        clamped, rooted, seq_sem = (new_semaphore(nc, m, (n)) for n in ("clamped", "rooted", "scale_seq"))
        with nc.Block() as block:
            @block.vector
            def _(dve):
                seq = Sequence(dve, seq_sem)
                nc.vector.tensor_scalar_max(m.isq_out[:, :], m.deg_out[:, :], 1.0).then_inc(clamped, 1)
                seq.link(nc.vector.tensor_scalar_max(m.degT[:, :], m.degT[:, :], 1.0))
                seq.link(nc.vector.reciprocal(m.degT[:, :], m.degT[:, :]))
                dve.wait_ge(rooted, 1)
                seq.link(nc.vector.reciprocal(m.isq_out[:, :], m.isq_out[:, :]))

            @block.scalar
            def _(act):
                act.wait_ge(clamped, 1)
                act.activation(m.isq_out[:, :], m.isq_out[:, :], ACT.Sqrt).then_inc(rooted, 1)



def normalise(nc, m, name, again=False):
    with ExitStack() as ph:
        def sb(n, shape, dt=F32):
            return ph.enter_context(nc.sbuf_tensor(f"{name}_{n}", shape, dt))

        def sem(n):
            return new_semaphore(nc, m, (f"{name}_{n}"))

        stats, moments = sb("stats", [P, NB, 6]), sb("moments", [P, NB, 2])
        std = sb("std", [P, NB])
        seq_sem, var_made, std_made, centred, relu_made = (
            sem(n) for n in ("dve_seq", "var_made", "std_made", "centred", "relu_made"))
        rows_made, T_ps, T_taken = (sem(n) for n in ("rows_made", "T_ps", "T_taken"))

        passes = 2 if again else 1
        with nc.Block() as block:
            @block.vector
            def _(dve):
                seq = Sequence(dve, seq_sem)
                for n in range(passes):
                    source = m.H if n else m.X
                    if n:
                        dve.wait_ge(relu_made, NGRP)
                    for b in range(NB):
                        seq.did(nc.vector.bn_stats(stats[:, b, :], source[:, b, :]))
                    seq.wait()
                    for b in range(NB):
                        seq.did(nc.vector.bn_aggr(moments[:, b, :], stats[:, b, :]))
                    seq.wait()
                    seq.link(nc.vector.tensor_copy(m.rstd[:, :], moments[:, :, 1]))
                    nc.vector.tensor_copy(std[:, :], m.rstd[:, :]).then_inc(var_made, 1)
                    dve.wait_ge(std_made, n + 1)
                    seq.link(nc.vector.reciprocal(m.rstd[:, :], std[:, :]))
                    for g in range(NGRP):
                        for b in range(g * GB, (g + 1) * GB):
                            last = nc.vector.tensor_scalar(m.D[:, b, :], source[:, b, :], moments[:, b, 0:1],
                                                           m.rstd[:, b:b + 1], ALU.subtract, ALU.mult)
                        last.then_inc(centred, 1)
                if again:
                    for g in range(NGRP):
                        dve.wait_ge(centred, NGRP + g + 1)
                        blocks = group_blocks(g)
                        bc = [v[:, :].rearrange("p (a f) -> p a f", a=1).to_broadcast([P, GB, FEAT])
                              for v in (m.gamma, m.beta)]
                        seq.link(nc.vector.tensor_tensor(m.D[:, blocks, :], m.D[:, blocks, :], bc[0], ALU.mult))
                        seq.link(nc.vector.tensor_tensor(m.H[:, blocks, :], m.D[:, blocks, :], bc[1], ALU.add))
                        for b in range(g * GB, (g + 1) * GB):
                            last = nc.vector.tensor_scalar(m.D[:, b, :], m.H[:, b, :], m.isq_out[:, b:b + 1], None,
                                                           ALU.mult)
                        last.then_inc(rows_made, 1)

            @block.scalar
            def _(act):
                for n in range(passes):
                    act.wait_ge(var_made, n + 1)
                    act.activation(std[:, :], std[:, :], ACT.Sqrt, bias=m.eps[:, 0:1]).then_inc(std_made, 1)
                    for g in range(NGRP if n == 0 else 0):
                        act.wait_ge(centred, g + 1)
                        act.activation(m.H[:, group_blocks(g), :], m.D[:, group_blocks(g), :], ACT.Relu)\
                           .then_inc(relu_made if again else rows_made, 1)
                        if again:
                            act.wait_ge(relu_made, g + 1)
                for g in range(NGRP):
                    act.wait_ge(T_ps, g + 1)
                    act.activation(m.HT[:, group_cols(g)].rearrange("p (b f) -> p b f", b=GB), node_group(m, g),
                                   ACT.Copy).then_inc(T_taken, 1)

            @block.tensor
            def _(pe):
                for g in range(NGRP):
                    pe.wait_ge(rows_made, g + 1)
                    if g >= 2:
                        pe.wait_ge(T_taken, g - 1)
                    for b in range(GB):
                        last = nc.tensor.transpose(node_bank(m, g, b), m.H[:, g * GB + b, :], m.ident[:, :])
                    last.then_inc(T_ps, 1)



def sum_neighbours(nc, m, name, rows, sums):
    with ExitStack() as ph:
        def sb(n, shape, dt=F32):
            return ph.enter_context(nc.sbuf_tensor(f"{name}_{n}", shape, dt))

        def sem(n):
            return new_semaphore(nc, m, (f"{name}_{n}"))

        got, hot = sb("got", [P, 2, GI, FEAT]), sb("hot", [P, 2, GI, P])
        idx_now = sb("idx_now", [P, 2, GI], I32)
        idx_staged, hot_made, summed, added, turns, rows_kept = (
            sem(n) for n in ("idx_staged", "hot_made", "summed", "added", "turns", "rows_kept"))
        got_in = [sem(f"got_in{p}") for p in range(2)]
        START = 4
        with nc.Block() as block:
            @block.sync
            def _(sp):
                with when_general(m, sp):
                    sp.dma_start(m.h_table.rearrange("(b p) f -> p b f", p=P), rows).then_inc(rows_kept, 16)

            @block.gpsimd
            def _(pool):
                with when_general(m, pool):
                    pool.wait_ge(rows_kept, 16)
                    pool.sem_inc(turns, 1)
                    with pool.Fori(0, NG // 2) as i:
                        for p in range(2):
                            pool.wait_ge(summed, i * 4 + 2 * p + 2)
                            pool.sem_inc(turns, 1)
                            nc.gpsimd.tensor_copy(idx_now[:, p, :], m.idx[:, bass.ds(i * 2 * GI + p * GI, GI)])\
                                .then_inc(idx_staged, 1)
                            pool.wait_ge(idx_staged, i * 2 + p + 1)
                            pool.sem_inc(turns, 1)
                            for j in range(GI):
                                pool.indirect_dma_start(
                                    out=got[:, p, j, :], out_offset=None, in_=m.h_table[:, :],
                                    in_offset=bass.IndirectOffsetOnAxis(ap=idx_now[:, p, j:j + 1], axis=0))\
                                    .then_inc(got_in[p], 16)

            @block.vector
            def _(dve):
                with when_general(m, dve):
                    nc.vector.memset(sums[:, :], 0.0).then_inc(added, 8)
                    with dve.Fori(0, NG // 2) as i:
                        for p in range(2):
                            blocks = loads(nc, dve, m.block_row, i * 2 * GI + p * GI, GI, NB - 1)
                            dve.wait_ge(summed, i * 4 + 2 * p + 2)
                            nc.vector.tensor_tensor(
                                hot[:, p, :, :],
                                m.iota_f[:, 0:P].rearrange("p (a w) -> p a w", a=1).to_broadcast([P, GI, P]),
                                m.rel[:, bass.ds(i * 2 * GI + p * GI, GI)].rearrange("p (t a) -> p t a", a=1)
                                .to_broadcast([P, GI, P]), ALU.is_equal).then_inc(hot_made, 1)
                            for half in range(2):
                                dve.wait_ge(summed, START + i * 4 + 2 * p + half + 1)
                                for j in range(4):
                                    done = i * 2 * GI + p * GI + half * 4 + j
                                    dve.wait_ge(added, 8 + done)
                                    cols = bass.ds(blocks[half * 4 + j] * P, P)
                                    nc.vector.tensor_tensor(sums[:, cols], sums[:, cols],
                                                            m.ps[:, 4 + half, j * P:(j + 1) * P], ALU.add)\
                                        .then_inc(added, 1)

            @block.tensor
            def _(pe):
                with when_general(m, pe):
                    pe.sem_inc(summed, START)
                    with pe.Fori(0, NG // 2) as i:
                        for p in range(2):
                            pe.wait_ge(hot_made, i * 2 + p + 1)
                            pe.wait_ge(got_in[p], (i + 1) * 16 * GI)
                            for half in range(2):
                                pe.wait_ge(added, i * 2 * GI + p * GI + 4 * (half + 1))
                                for j in range(4):
                                    last = nc.tensor.matmul(m.ps[:, 4 + half, j * P:(j + 1) * P],
                                                            got[:, p, half * 4 + j, :], hot[:, p, half * 4 + j, :],
                                                            start=True, stop=True)
                                last.then_inc(summed, 1)



def project_pair(nc, m, name, self_w, agg_w, bias, root):
    with ExitStack() as ph:
        def sem(n):
            return new_semaphore(nc, m, (f"{name}_{n}"))

        product, taken, scaled, rooted = (sem(n) for n in ("product", "taken", "scaled", "rooted"))
        with nc.Block() as block:
            @block.scalar
            def _(act):
                if root:
                    act.activation(m.degT[:, :], m.degT[:, :], ACT.Sqrt).then_inc(rooted, 1)

            @block.tensor
            def _(pe):
                for g in range(NGRP):
                    pe.wait_ge(scaled, g + 1)
                    if g >= 2:
                        pe.wait_ge(taken, g - 1)
                    for b in range(GB):
                        cols = slice((g * GB + b) * P, (g * GB + b + 1) * P)
                        bank = node_bank(m, g, b)
                        nc.tensor.matmul(bank, m.HT[:, cols], self_w[:, :], start=True, stop=False)
                        nc.tensor.matmul(bank, m.AGGT[:, cols], agg_w[:, :], start=False, stop=False)
                        last = nc.tensor.matmul(bank, m.ones[0:1, :], bias[0:1, :], start=False, stop=True)
                    last.then_inc(product, 1)

            @block.vector
            def _(dve):
                if root:
                    dve.wait_ge(rooted, 1)
                for g in range(NGRP):
                    nc.vector.tensor_tensor(m.AGGT[:, group_cols(g)], m.AGGT[:, group_cols(g)],
                                            m.degT[:, group_cols(g)], ALU.mult).then_inc(scaled, 1)
                for g in range(NGRP):
                    dve.wait_ge(product, g + 1)
                    blocks = group_blocks(g)
                    nc.vector.tensor_tensor(m.X[:, blocks, :], m.X[:, blocks, :], node_group(m, g), ALU.add)\
                        .then_inc(taken, 1)


def project_sum(nc, m):
    with ExitStack() as ph:
        def sem(n):
            return new_semaphore(nc, m, (f"l1_{n}"))

        summed, product, taken = sem("summed"), sem("product"), sem("taken")
        with nc.Block() as block:
            @block.gpsimd
            def _(pool):
                for g in range(NGRP):
                    nc.gpsimd.tensor_tensor(m.HT[:, group_cols(g)], m.HT[:, group_cols(g)], m.AGGT[:, group_cols(g)],
                                            ALU.add).then_inc(summed, 1)

            @block.tensor
            def _(pe):
                for g in range(NGRP):
                    pe.wait_ge(summed, g + 1)
                    if g >= 2:
                        pe.wait_ge(taken, g - 1)
                    for b in range(GB):
                        cols = slice((g * GB + b) * P, (g * GB + b + 1) * P)
                        last = nc.tensor.matmul(node_bank(m, g, b), m.HT[:, cols], m.W["W1"][:, :],
                                                start=True, stop=True)
                    last.then_inc(product, 1)

            @block.vector
            def _(dve):
                for g in range(NGRP):
                    dve.wait_ge(product, g + 1)
                    blocks = group_blocks(g)
                    nc.vector.scalar_tensor_tensor(m.X[:, blocks, :], node_group(m, g), 0.0, m.X[:, blocks, :],
                                                   ALU.max, ALU.add).then_inc(taken, 1)



def project_qkv(nc, m, Q3):
    with ExitStack() as ph:
        def sem(n):
            return new_semaphore(nc, m, (f"qkv_{n}"))

        kv_rows = ph.enter_context(nc.sbuf_tensor("kv_rows", [P, 2, GB, 2, FEAT], F32))
        q_rest = ph.enter_context(nc.sbuf_tensor("q_rest", [P, GB, FEAT], F32))
        product, q_taken, kv_taken, seq_sem = (sem(n) for n in ("product", "q_taken", "kv_taken", "dve_seq"))
        kept = [sem(f"kv_kept{p}") for p in range(2)]
        names = ("k", "v", "q")
        with nc.Block() as block:
            @block.tensor
            def _(pe):
                for n in range(3 * NGRP):
                    g, what = n // 3, names[n % 3]
                    if n >= 2:
                        before = n - 2
                        if before % 3 == 2:
                            pe.wait_ge(q_taken, before // 3 + 1)
                        else:
                            pe.wait_ge(kv_taken, before // 3 * 2 + before % 3 + 1)
                    for b in range(GB):
                        cols = slice((g * GB + b) * P, (g * GB + b + 1) * P)
                        nc.tensor.matmul(node_bank(m, n, b), m.HT[:, cols], m.W["W" + what][:, :],
                                         start=True, stop=False)
                        last = nc.tensor.matmul(node_bank(m, n, b), m.ones[0:1, :], m.brow["b" + what][0:1, :],
                                                start=False, stop=True)
                    last.then_inc(product, 1)

            @block.scalar
            def _(act):
                for g in range(NGRP):
                    if g >= 2:
                        act.wait_ge(kept[g % 2], 16 * (g // 2))
                    for k in range(2):
                        act.wait_ge(product, 3 * g + k + 1)
                        act.activation(kv_rows[:, g % 2, :, k, :], node_group(m, 3 * g + k), ACT.Copy)\
                           .then_inc(kv_taken, 1)

            @block.sync
            def _(sp):
                for g in range(NGRP):
                    sp.wait_ge(kv_taken, 2 * g + 2)
                    sp.dma_start(m.kv_table[g * GB * P:(g + 1) * GB * P, :].rearrange("(b p) f -> p b f", p=P),
                                 kv_rows[:, g % 2, :, :, :].rearrange("p b k f -> p b (k f)"))\
                        .then_inc(kept[g % 2], 16)
                sp.wait_ge(kept[0], 16 * ((NGRP + 1) // 2))
                sp.wait_ge(kept[1], 16 * (NGRP // 2))

            @block.vector
            def _(dve):
                seq = Sequence(dve, seq_sem)
                for g in range(NGRP):
                    dve.wait_ge(product, 3 * g + 3)
                    q = node_group(m, 3 * g + 2)
                    parts = [Q3[:, group_blocks(g), k, :] for k in range(3)]
                    seq.link(nc.vector.tensor_copy(parts[0], q))
                    nc.vector.tensor_tensor(q_rest[:, :, :], q, parts[0], ALU.subtract).then_inc(q_taken, 1)
                    dve.wait_ge(q_taken, g + 1)
                    seq.link(nc.vector.tensor_copy(parts[1], q_rest[:, :, :]))
                    seq.link(nc.vector.tensor_tensor(q_rest[:, :, :], q_rest[:, :, :], parts[1], ALU.subtract))
                    seq.link(nc.vector.tensor_copy(parts[2], q_rest[:, :, :]))


def score_edges(nc, m, Q3):
    GL = 4
    with ExitStack() as ph:
        def sb(n, shape, dt=F32):
            return ph.enter_context(nc.sbuf_tensor(f"sc_{n}", shape, dt))

        def sem(n):
            return new_semaphore(nc, m, (f"sc_{n}"))

        kv, ea = sb("kv", [P, GL, GI, 2, FEAT]), sb("ea", [EDIM, GL, GI, P])
        idx_now = sb("idx_now", [P, GL, GI], I32)
        hot, hotT = sb("hot", [P, 2, GI, P], BF16), sb("hotT", [P, 2, GI, P], BF16)
        prod = sb("prod", [P, 2, 4, FEAT])
        hotT_ps = m.ps16
        turns, idx_staged, hot_made, turned, hotT_made, terms, edged, multiplied, scored = (
            sem(n) for n in ("turns", "idx_staged", "hot_made", "turned", "hotT_made", "terms", "edged", "multiplied",
                             "scored"))
        kv_in, spilled = ([sem(f"{n}{q}") for q in range(GL)] for n in ("kv_in", "spilled"))
        ea_in = [sem(f"ea_in{q}") for q in range(GL)]
        STEPS = NG // GL

        def one_hot(first, p):
            return nc.vector.tensor_tensor(
                hot[:, p, :, :],
                m.iota_f[:, 0:P].rearrange("p (a w) -> p a w", a=1).to_broadcast([P, GI, P]),
                m.rel[:, bass.ds(first, GI)].rearrange("p (t a) -> p t a", a=1).to_broadcast([P, GI, P]),
                ALU.is_equal).then_inc(hot_made, 1)

        with nc.Block() as block:
            @block.gpsimd
            def _(pool):
                with pool.Fori(0, STEPS) as i:
                    for q in range(GL):
                        pool.wait_ge(spilled[q], i * 16 + 16)
                        pool.sem_inc(turns, 1)
                        nc.gpsimd.tensor_copy(idx_now[:, q, :], m.idx[:, bass.ds(i * GL * GI + q * GI, GI)])\
                            .then_inc(idx_staged, 1)
                        pool.wait_ge(idx_staged, i * GL + q + 1)
                        pool.sem_inc(turns, 1)
                        for j in range(GI):
                            pool.indirect_dma_start(
                                out=kv[:, q, j, :, :].rearrange("p k f -> p (k f)"), out_offset=None,
                                in_=m.kv_table[:, :],
                                in_offset=bass.IndirectOffsetOnAxis(ap=idx_now[:, q, j:j + 1], axis=0))\
                                .then_inc(kv_in[q], 16)

            @block.scalar
            def _(act):
                with act.Fori(0, STEPS) as i:
                    for q in range(GL):
                        p = q % 2
                        act.wait_ge(turned, i * GL + q + 3)
                        act.activation(hotT[:, p, :, :], hotT_ps[:, p, :].rearrange("p (j e) -> p j e", j=GI),
                                       ACT.Copy).then_inc(hotT_made, 1)

            @block.vector
            def _(dve):
                one_hot(0, 0)
                one_hot(GI, 1)
                with dve.Fori(0, STEPS) as i:
                    for q in range(GL):
                        p = q % 2
                        dve.wait_ge(kv_in[q], i * (16 * GI) + 16 * GI)
                        for half in range(2):
                            n = i * GL * 2 + 2 * q + half
                            js = slice(4 * half, 4 * half + 4)
                            dve.wait_ge(terms, n + 5)
                            e = m.ps[:, 4 + half, :].rearrange("p (j a f) -> p j a f", j=4, a=1)\
                                .to_broadcast([P, 4, 2, FEAT])
                            nc.vector.tensor_tensor(kv[:, q, js, :, :], kv[:, q, js, :, :], e, ALU.add)\
                                .then_inc(edged, 1)
                            dve.wait_ge(edged, n + 1)
                            nc.vector.tensor_tensor(
                                prod[:, half, :, :], kv[:, q, js, 0, :],
                                m.ps[:, 2 + half, :].rearrange("p (j f) -> p j f", j=4), ALU.mult)\
                                .then_inc(multiplied, 1)
                            dve.wait_ge(multiplied, n + 3)
                            at = m.ALPHA[:, bass.ds(i, 1), :, q * GI + 4 * half:q * GI + 4 * half + 4]
                            nc.vector.tensor_reduce(
                                at.rearrange("p a h j -> p j (a h)"),
                                prod[:, half, :, :].rearrange("p j (h c) -> p j h c", h=HEADS), AX, ALU.add)\
                                .then_inc(scored, 1)
                        dve.wait_ge(turned, i * GL + q + 3)
                        one_hot(i * GL * GI + (q + 2) * GI, p)

            @block.sync
            def _(sp):
                for q in range(GL):
                    sp.sem_inc(spilled[q], 16)
                def load_edges(first, q):
                    tiles = loads(nc, sp, m.tile_row, first, GI, TILES - 1)
                    for j in range(GI):
                        sp.dma_start(ea[:, q, j, :], m.ea_tiles[bass.ds(tiles[j], 1), :, :]
                                     .rearrange("a c e -> (a c) e")).then_inc(ea_in[q], 16)

                load_edges(0, 0)
                load_edges(GI, 1)
                with sp.Fori(0, STEPS) as i:
                    for q in range(GL):
                        sp.wait_ge(terms, i * GL * 2 + 2 * q + 1)
                        load_edges(i * GL * GI + (q + 2) * GI, (q + 2) % GL)
                        sp.wait_ge(multiplied, i * GL * 2 + 2 * q + 4)
                        sp.dma_start(m.vj_spill[bass.ds(i * GL + q, 1), :, :]
                                     .rearrange("a p (j f) -> (a p) j f", j=GI), kv[:, q, :, 1, :])\
                            .then_inc(spilled[q], 16)
                for q in range(GL):
                    sp.wait_ge(spilled[q], STEPS * 16 + 16)
                    sp.wait_ge(ea_in[q], (STEPS + (q < 2)) * 16 * GI)

            @block.tensor
            def _(pe):
                def turn(p):
                    for j in range(GI):
                        last = nc.tensor.transpose(hotT_ps[:, p, j * P:(j + 1) * P], hot[:, p, j, :],
                                                   m.ident16[:, :])
                    last.then_inc(turned, 1)

                def half_terms(q, half, blocks):
                    p = q % 2
                    for j in range(4):
                        jj = 4 * half + j
                        cols = slice(j * P, (j + 1) * P)
                        nc.tensor.matmul(m.ps[:, 4 + half, cols], ea[:, q, jj, :], m.We[:, :], start=True, stop=True)
                        for k in range(3):
                            last = nc.tensor.matmul(
                                m.ps[:, 2 + half, cols], hotT[:, p, jj, :],
                                Q3[:, bass.ds(blocks[jj], 1), k, :].rearrange("p a f -> p (a f)"),
                                start=k == 0, stop=k == 2)
                    last.then_inc(terms, 1)

                pe.sem_inc(turned, 2)
                pe.sem_inc(terms, 4)
                pe.sem_inc(hotT_made, 2)
                pe.sem_inc(multiplied, 2)
                pe.wait_ge(hot_made, 1)
                turn(0)
                with pe.Fori(0, STEPS) as i:
                    for q in range(GL):
                        p = q % 2
                        blocks = loads(nc, pe, m.block_row, i * GL * GI + q * GI, GI, NB - 1)
                        pe.wait_ge(ea_in[q], i * (16 * GI) + 16 * GI)
                        pe.wait_ge(hotT_made, i * GL + q + 3)
                        pe.wait_ge(multiplied, i * GL * 2 + 2 * q + 1)
                        half_terms(q, 0, blocks)
                        pe.wait_ge(hot_made, i * GL + q + 2)
                        pe.wait_ge(hotT_made, i * GL + q + 2)
                        turn(1 - p)
                        pe.wait_ge(multiplied, i * GL * 2 + 2 * q + 2)
                        half_terms(q, 1, blocks)


def transpose_blocks(nc, m, pe, source, ready, taken, identity):
    groups = -(-IB // 4)
    for g in range(groups):
        if g >= 4:
            pe.wait_ge(taken, g - 3)
        for b in range(g * 4, min(g * 4 + 4, IB)):
            last = nc.tensor.transpose(m.ps[:, g % 4, (b % 4) * P:(b % 4 + 1) * P], source(b), identity)
        last.then_inc(ready, 1)


def softmax_edges(nc, m):
    with ExitStack() as ph:
        def sb(n, shape, dt=F32):
            return ph.enter_context(nc.sbuf_tensor(f"sm_{n}", shape, dt))

        def sem(n):
            return new_semaphore(nc, m, (f"sm_{n}"))

        turned = m.D
        chunk, invalid = sb("chunk", [P, CHUNK]), sb("invalid", [P, CHUNK])
        marks = [sb(n, [P, CHUNK]) for n in ("first", "last")]
        best = [sb(n, [P, CHUNK]) for n in ("forward", "backward")]
        ends = sb("ends", [P, 2, 2])
        end_rows = sb("end_rows", [1, 4, P])
        carry_rows = sb("carry_rows", [1, 2, P])
        carry = sb("carry", [P, 2])
        T_ps, T_taken, T_out, alpha_in, marks_in, seq_sem = (
            sem(n) for n in ("T_ps", "T_taken", "T_out", "alpha_in", "marks_in", "dve_seq"))
        ends_made, ends_ps, carry_made, carry_ps, maxed, exp_made, exp_out, exp_in, back_ps, back_taken = (
            sem(n) for n in ("ends_made", "ends_ps", "carry_made", "carry_ps", "maxed", "exp_made", "exp_out",
                             "exp_in", "back_ps", "back_taken"))
        groups = -(-IB // 4)

        def bank(g):
            n = min(4, IB - g * 4)
            return m.ps[:, g % 4, 0:n * P].rearrange("p (b e) -> p b e", b=n), slice(g * 4, g * 4 + n)

        def by_item(dram_row):
            return dram_row.rearrange("(b i e) -> i b e", i=32, e=P)

        with nc.Block() as block:
            @block.tensor
            def _(pe):
                transpose_blocks(nc, m, pe, lambda b: m.ALPHA[:, b, :, :].rearrange("p h i -> p (h i)"),
                                 T_ps, T_taken, m.ident[:, :])
                pe.wait_ge(ends_made, 1)
                for k in range(4):
                    last = nc.tensor.transpose(m.ps[0:1, 4, k * P:(k + 1) * P], ends[:, k // 2, k % 2:k % 2 + 1],
                                               m.ident[:, :])
                last.then_inc(ends_ps, 1)
                pe.wait_ge(carry_made, 1)
                for k in range(2):
                    last = nc.tensor.transpose(m.ps[:, 5, k:k + 1], carry_rows[0:1, k, :], m.ident[0:1, 0:1])
                last.then_inc(carry_ps, 1)
                pe.wait_ge(exp_in, 16 * HEADS)
                transpose_blocks(nc, m, pe, lambda b: turned[:, b, :], back_ps, back_taken, m.ident[:, :])

            @block.scalar
            def _(act):
                for g in range(groups):
                    act.wait_ge(T_ps, g + 1)
                    src, blocks = bank(g)
                    act.activation(turned[:, blocks, :], src, ACT.Copy).then_inc(T_taken, 1)
                act.wait_ge(maxed, 1)
                act.activation(chunk[:, :], chunk[:, :], ACT.Exp, scale=float(CH) ** -0.5).then_inc(exp_made, 1)
                for g in range(groups):
                    act.wait_ge(back_ps, g + 1)
                    src, blocks = bank(g)
                    act.activation(m.ALPHA[:, blocks, :, :].rearrange("p b h i -> p b (h i)"), src, ACT.Copy)\
                       .then_inc(back_taken, 1)

            @block.sync
            def _(sp):
                for k, tile in enumerate((*marks, invalid)):
                    for h in range(HEADS):
                        sp.dma_start(tile[h * CHUNKS:(h + 1) * CHUNKS, :],
                                     m.marks_dram[k].rearrange("(c n) -> c n", c=CHUNKS)).then_inc(marks_in, 16)
                sp.wait_ge(T_taken, groups)
                for h in range(HEADS):
                    sp.dma_start(by_item(m.alpha_dram[h]), turned[h * 32:(h + 1) * 32, :, :]).then_inc(T_out, 16)
                sp.wait_ge(T_out, 16 * HEADS)
                sp.dma_start(chunk[:, :], m.alpha_dram.rearrange("h (c n) -> (h c) n", c=CHUNKS))\
                    .then_inc(alpha_in, 16)
                sp.wait_ge(exp_made, 1)
                sp.dma_start(m.ex_dram.rearrange("h (c n) -> (h c) n", c=CHUNKS), chunk[:, :]).then_inc(exp_out, 16)
                sp.wait_ge(exp_out, 16)
                for h in range(HEADS):
                    sp.dma_start(turned[h * 32:(h + 1) * 32, :, :], by_item(m.ex_dram[h])).then_inc(exp_in, 16)

            @block.vector
            def _(dve):
                seq = Sequence(dve, seq_sem)
                dve.wait_ge(marks_in, 16 * 3 * HEADS)
                for k in range(2):
                    seq.did(nc.vector.tensor_reduce(ends[:, k, 1:2], marks[k][:, :], AX, ALU.min))
                seq.did(nc.vector.memset(carry_rows[:, :, :], -BIG))
                dve.wait_ge(alpha_in, 16)
                seq.link(nc.vector.tensor_tensor(chunk[:, :], chunk[:, :], invalid[:, :], ALU.add))

                def scan(k, start):
                    way = slice(None, None, -1) if k else slice(None)
                    return nc.vector.tensor_tensor_scan(best[k][:, way], marks[k][:, way], chunk[:, way], start,
                                                        ALU.add, ALU.max)

                seq.did(scan(0, -BIG))
                seq.link(scan(1, -BIG))
                seq.did(nc.vector.tensor_copy(ends[:, 0, 0:1], best[0][:, CHUNK - 1:CHUNK]))
                nc.vector.tensor_copy(ends[:, 1, 0:1], best[1][:, 0:1]).then_inc(ends_made, 1)
                dve.wait_ge(ends_ps, 1)
                seq.link(nc.vector.tensor_copy(end_rows[:, :, :], m.ps[0:1, 4, :].rearrange("a (k p) -> a k p", k=4)))
                seq.did(nc.vector.memset(end_rows[0:1, 0:2, CHUNKS - 1::CHUNKS], -BIG))
                seq.link(nc.vector.memset(end_rows[0:1, 2:4, 0::CHUNKS], -BIG))
                seq.did(nc.vector.tensor_tensor_scan(carry_rows[0:1, 0, 1:P], end_rows[0:1, 1, 0:P - 1],
                                                     end_rows[0:1, 0, 0:P - 1], -BIG, ALU.add, ALU.max))
                nc.vector.tensor_tensor_scan(carry_rows[0:1, 1, 0:P - 1][:, ::-1], end_rows[0:1, 3, 1:P][:, ::-1],
                                             end_rows[0:1, 2, 1:P][:, ::-1], -BIG, ALU.add, ALU.max)\
                    .then_inc(carry_made, 1)
                dve.wait_ge(carry_ps, 1)
                seq.link(nc.vector.tensor_copy(carry[:, :], m.ps[:, 5, 0:2]))
                seq.did(scan(0, carry[:, 0:1]))
                seq.link(scan(1, carry[:, 1:2]))
                seq.link(nc.vector.tensor_tensor(best[0][:, :], best[0][:, :], best[1][:, :], ALU.max))
                nc.vector.tensor_tensor(chunk[:, :], chunk[:, :], best[0][:, :], ALU.subtract).then_inc(maxed, 1)


def weigh_edges(nc, m):
    WIDE = FEAT + HEADS
    with ExitStack() as ph:
        def sb(n, shape, dt=F32):
            return ph.enter_context(nc.sbuf_tensor(f"we_{n}", shape, dt))

        def sem(n):
            return new_semaphore(nc, m, (f"we_{n}"))

        vj, msg, hot = sb("vj", [P, 2, GI, FEAT]), sb("msg", [P, 2, GI, WIDE]), sb("hot", [P, 2, GI, P])
        rel_now = sb("rel_now", [P, GI])
        hot_made, weighed, msg_made, rel_staged, apart, act_hot, summed, added = (
            sem(n) for n in ("hot_made", "weighed", "msg_made", "rel_staged", "apart", "act_hot", "summed", "added"))
        ON_DVE = 4
        vj_in = [sem(f"vj_in{p}") for p in range(2)]
        GL = 4
        STEPS = NG // GL

        def exponentials(i, q):
            return m.ALPHA[:, bass.ds(i, 1), :, q * GI:(q + 1) * GI]

        def one_hot(first, p):
            nc.vector.tensor_tensor(
                hot[:, p, 0:ON_DVE, :],
                m.iota_f[:, 0:P].rearrange("p (a w) -> p a w", a=1).to_broadcast([P, ON_DVE, P]),
                m.rel[:, bass.ds(first, ON_DVE)].rearrange("p (t a) -> p t a", a=1).to_broadcast([P, ON_DVE, P]),
                ALU.is_equal).then_inc(hot_made, 1)

        def out_ps(half, j):
            return m.ps[:, 4 + 2 * half + j // 2, (j % 2) * WIDE:(j % 2 + 1) * WIDE]

        with nc.Block() as block:
            @block.sync
            def _(sp):
                with sp.Fori(0, NG // 2) as i:
                    for p in range(2):
                        sp.wait_ge(weighed, i * 2 + p + 1)
                        sp.dma_start(vj[:, p, :, :].rearrange("p j f -> p (j f)"),
                                     m.vj_spill[bass.ds(i * 2 + p, 1), :, :].rearrange("a p n -> (a p) n"))\
                            .then_inc(vj_in[p], 16)

            @block.gpsimd
            def _(pool):
                pool.sem_inc(weighed, 2)
                with pool.Fori(0, STEPS) as i:
                    for q in range(GL):
                        p = q % 2
                        pool.wait_ge(summed, i * 2 * GL + 2 * q + 2)
                        pool.wait_ge(vj_in[p], i * (GL // 2 * 16) + (q // 2 + 1) * 16)
                        nc.gpsimd.tensor_tensor(
                            msg[:, p, :, 0:FEAT].rearrange("p j (h c) -> p j h c", h=HEADS),
                            vj[:, p, :, :].rearrange("p j (h c) -> p j h c", h=HEADS),
                            exponentials(i, q).rearrange("p a h (j c) -> p j (a h) c", c=1)
                            .to_broadcast([P, GI, HEADS, CH]), ALU.mult).then_inc(weighed, 1)

            @block.scalar
            def _(act):
                with act.Fori(0, STEPS) as i:
                    for q in range(GL):
                        act.wait_ge(summed, i * 2 * GL + 2 * q + 2)
                        nc.scalar.activation(msg[:, q % 2, :, FEAT:WIDE],
                                             exponentials(i, q).rearrange("p a h j -> p j (a h)"), ACT.Copy)\
                            .then_inc(msg_made, 1)
                        nc.scalar.activation(rel_now[:, :], m.rel[:, bass.ds(i * GL * GI + q * GI, GI)], ACT.Copy)\
                            .then_inc(rel_staged, 1)
                        act.wait_ge(rel_staged, i * GL + q + 1)
                        for j in range(ON_DVE, GI):
                            last = nc.scalar.activation(hot[:, q % 2, j, :], m.iota_f[:, 0:P], ACT.Abs,
                                                        scale=-1.0, bias=rel_now[:, j:j + 1])
                        last.then_inc(apart, 1)
                        act.wait_ge(apart, i * GL + q + 1)
                        nc.scalar.activation(hot[:, q % 2, ON_DVE:GI, :], hot[:, q % 2, ON_DVE:GI, :], ACT.Relu,
                                             scale=-1.0, bias=m.ones[:, 0:1]).then_inc(act_hot, 1)

            @block.vector
            def _(dve):
                one_hot(0, 0)
                nc.vector.memset(m.ACC[:, :, :, :], 0.0).then_inc(added, 8)
                with dve.Fori(0, NG // 2) as i:
                    for p in range(2):
                        first = i * 2 * GI + p * GI
                        one_hot(first + GI, 1 - p)
                        blocks = loads(nc, dve, m.block_row, first, GI, NB - 1)
                        for half in range(2):
                            dve.wait_ge(summed, 4 + i * 4 + 2 * p + half + 1)
                            for j in range(4):
                                jj = half * 4 + j
                                dve.wait_ge(added, 8 + first + jj - 1)
                                at = m.ACC[:, j % 2, bass.ds(blocks[jj], 1), :].rearrange("p a f -> p (a f)")
                                nc.vector.tensor_tensor(at, at, out_ps(half, j), ALU.add).then_inc(added, 1)

            @block.tensor
            def _(pe):
                pe.sem_inc(summed, 4)
                with pe.Fori(0, NG // 2) as i:
                    for p in range(2):
                        pe.wait_ge(hot_made, i * 2 + p + 1)
                        pe.wait_ge(weighed, i * 2 + p + 3)
                        pe.wait_ge(msg_made, i * 2 + p + 1)
                        pe.wait_ge(act_hot, i * 2 + p + 1)
                        for half in range(2):
                            pe.wait_ge(added, i * 2 * GI + p * GI + 4 * (half + 1))
                            for j in range(4):
                                last = nc.tensor.matmul(out_ps(half, j), hot[:, p, half * 4 + j, :],
                                                        msg[:, p, half * 4 + j, :], start=True, stop=True)
                            last.then_inc(summed, 1)


def finish_attention(nc, m):
    with ExitStack() as ph:
        def sb(n, shape, dt=F32):
            return ph.enter_context(nc.sbuf_tensor(f"fa_{n}", shape, dt))

        def sem(n):
            return new_semaphore(nc, m, (f"fa_{n}"))

        rden = sb("rden", [P, NB, HEADS])
        total = m.ACC[:, 0, :, :]
        seq_sem, product, act_taken, dve_taken = (sem(n) for n in ("dve_seq", "product", "act_taken", "dve_taken"))
        stages = ("skip", "turn", "mlp1", "mlp2", "back")
        on_act = ("turn", "mlp1", "mlp2")
        order = [(s, g) for s in stages for g in range(NGRP)]

        def count(n, act):
            return sum((order[k][0] in on_act) == act for k in range(n + 1))

        with nc.Block() as block:
            @block.tensor
            def _(pe):
                for n, (stage, g) in enumerate(order):
                    if n >= 2:
                        act = order[n - 2][0] in on_act
                        pe.wait_ge(act_taken if act else dve_taken, count(n - 2, act))
                    if stage != "skip":
                        act = order[n - NGRP][0] in on_act
                        pe.wait_ge(act_taken if act else dve_taken, count(n - NGRP, act))
                    for b in range(GB):
                        at = g * GB + b
                        cols = slice(at * P, (at + 1) * P)
                        bank = node_bank(m, n, b)
                        if stage == "skip":
                            nc.tensor.matmul(bank, m.HT[:, cols], m.W["Wskip"][:, :], start=True, stop=False)
                            last = nc.tensor.matmul(bank, m.ones[0:1, :], m.brow["bskip"][0:1, :],
                                                    start=False, stop=True)
                        elif stage == "turn":
                            last = nc.tensor.transpose(bank, m.D[:, at, :], m.ident[:, :])
                        elif stage == "mlp1":
                            last = nc.tensor.matmul(bank, m.W["M1"][:, :], m.AGGT[:, cols], start=True, stop=True)
                        elif stage == "mlp2":
                            last = nc.tensor.matmul(bank, m.W["M2"][:, :], m.HT[:, cols], start=True, stop=True)
                        else:
                            last = nc.tensor.transpose(bank, m.AGGT[:, cols], m.ident[:, :])
                    last.then_inc(product, 1)

            @block.scalar
            def _(act):
                for n, (stage, g) in enumerate(order):
                    if stage not in on_act:
                        continue
                    act.wait_ge(product, n + 1)
                    out = (m.HT if stage == "mlp1" else m.AGGT)[:, group_cols(g)]\
                        .rearrange("p (b f) -> p b f", b=GB)
                    if stage == "turn":
                        act.activation(out, node_group(m, n), ACT.Copy).then_inc(act_taken, 1)
                    else:
                        bias = m.b1col if stage == "mlp1" else m.b2col
                        act.activation(out, node_group(m, n), ACT.Gelu_apprx_tanh, bias=bias[:, 0:1])\
                           .then_inc(act_taken, 1)

            @block.vector
            def _(dve):
                seq = Sequence(dve, seq_sem)
                seq.link(nc.vector.tensor_tensor(total, m.ACC[:, 0, :, :], m.ACC[:, 1, :, :], ALU.add))
                seq.link(nc.vector.tensor_scalar_add(rden[:, :, :], total[:, :, FEAT:FEAT + HEADS], 1e-16))
                seq.link(nc.vector.reciprocal(rden[:, :, :], rden[:, :, :]))
                for h in range(HEADS):
                    seq.did(nc.vector.tensor_tensor(m.D[:, 0:NB, h * CH:(h + 1) * CH], total[:, :, h * CH:(h + 1) * CH],
                                                    rden[:, :, h:h + 1].to_broadcast([P, NB, CH]), ALU.mult))
                seq.wait()
                done = 0
                for n, (stage, g) in enumerate(order):
                    if stage in on_act:
                        continue
                    dve.wait_ge(product, n + 1)
                    blocks = group_blocks(g)
                    if stage == "skip":
                        nc.vector.tensor_tensor(m.D[:, blocks, :], m.D[:, blocks, :], node_group(m, n), ALU.add)\
                            .then_inc(dve_taken, 1)
                        done += 1
                        dve.wait_ge(dve_taken, done)
                        seq.did(nc.vector.tensor_tensor(m.X[:, blocks, :], m.X[:, blocks, :], m.D[:, blocks, :],
                                                        ALU.add))
                    else:
                        if g == 0:
                            seq.wait()
                        nc.vector.tensor_tensor(m.X[:, blocks, :], m.X[:, blocks, :], node_group(m, n), ALU.add)\
                            .then_inc(dve_taken, 1)


def store_output(nc, m, out):
    with ExitStack() as ph:
        stored = new_semaphore(nc, m, ("stored"))
        with nc.Block() as block:
            @block.sync
            def _(sp):
                sp.dma_start(out[0:FULL * P, :].rearrange("(b p) f -> p b f", p=P), m.X[:, 0:FULL, :])\
                    .then_inc(stored, 16)
                sp.dma_start(out[FULL * P:NODES, :], m.X[0:LAST, FULL, :]).then_inc(stored, 16)
                sp.wait_ge(stored, 32)


def build(nc, t, out):
    with ExitStack() as ctx:
        def sb(name, shape, dt=F32):
            return ctx.enter_context(nc.sbuf_tensor(name, shape, dt))

        def dram(name, shape):
            return nc.dram_tensor(name, shape, F32, kind="Internal").ap()

        m = Memory()
        m.semaphores = []
        m.h_table = dram("h_table", [NB * P, FEAT])
        m.kv_table = dram("kv_table", [NB * P, 2 * FEAT])
        m.vj_spill = dram("vj_spill", [NG, P, GI * FEAT])
        m.alpha_dram = dram("alpha_dram", [HEADS, NI * P])
        m.ex_dram = dram("ex_dram", [HEADS, NI * P])
        m.marks_dram = dram("marks_dram", [3, NI * P])
        m.adj_dram = nc.dram_tensor("adj_dram", [CHK, P, NB * CW], BF16, kind="Internal").ap()
        m.ea_tiles = t["ea_tiles"]
        m.rel = sb("rel", [P, NI + 2 * GI])
        m.idx = sb("idx", [P, NI], I32)
        m.block_row = sb("block_row", [1, NI], I32)
        m.tile_row = sb("tile_row", [1, NI + 2 * GI], I32)
        m.iota_f = sb("iota_f", [P, NI])
        m.pid_f = sb("pid_f", [P, KB])
        m.ones = sb("ones", [P, P])
        m.eps = sb("eps", [P, 1])

        def psum(ph, name, shape, dt=F32):
            return ph.enter_context(nc.psum_tensor(name, shape, dt))

        with ExitStack() as ph:
            m.ps = psum(ph, "ps_build", [P, 8, 512])
            make_constants(nc, m)
            list_items(nc, m, t)
            with ExitStack() as building:
                m.key = building.enter_context(nc.sbuf_tensor("key", [P, 2, NA + 8], BF16))
                m.low = building.enter_context(nc.sbuf_tensor("low7", [P, 2, NA + 8], BF16))
                m.group_row = building.enter_context(nc.sbuf_tensor("group_row", [1, NA], I32))
                list_adjacency_items(nc, m, t)
                build_adjacency(nc, m)
            clear_semaphores(nc, m)

        m.ident = sb("ident", [P, P])
        m.ident16 = sb("ident16", [P, P], BF16)
        m.ones16 = sb("ones16", [P, P], BF16)
        m.X = sb("X", [P, NB, FEAT])
        m.H = sb("H", [P, NB, FEAT])
        m.D = sb("D", [P, IB, FEAT])
        m.HT = sb("HT", [P, NB * P])
        m.AGGT = sb("AGGT", [P, NB * P])
        m.degT = sb("degT", [P, NB * P])
        m.rstd = sb("rstd", [P, NB])
        m.deg_out = sb("deg_out", [P, NB])
        m.isq_out = sb("isq_out", [P, NB])
        m.most = sb("most", [1, 1])
        m.general = sb("general", [1, 1], I32)
        m.W = {n: sb("w_" + n, [P, FEAT]) for n in ("W0a", "W0b", "W1", "Wq", "Wk", "Wv", "Wskip", "M1", "M2",
                                                    "W3a", "W3b")}
        m.We = sb("w_We", [EDIM, FEAT])
        m.brow = {n: sb("r_" + n, [1, FEAT]) for n in ("b0", "bq", "bk", "bv", "bskip", "b3")}
        m.b1col = sb("b1col", [P, 1])
        m.b2col = sb("b2col", [P, 1])
        m.gamma = sb("gamma", [P, FEAT])
        m.beta = sb("beta", [P, FEAT])

        with ExitStack() as ph:
            m.ps = psum(ph, "ps", [P, 8, 512])
            load_inputs(nc, m, t)

            normalise(nc, m, "n0")
            apply_adjacency(nc, m, "a0", m.H, degrees=True)
            sum_neighbours(nc, m, "deg", m.ones[:, :].rearrange("p (a f) -> p a f", a=1)
                           .to_broadcast([P, NB, FEAT]), m.degT)
            count_sources(nc, m, t)
            sum_neighbours(nc, m, "s0", m.H[:, :, :], m.AGGT)
            scale_degrees(nc, m)
            project_pair(nc, m, "p0", m.W["W0a"], m.W["W0b"], m.brow["b0"], root=False)

            clear_semaphores(nc, m)
            normalise(nc, m, "n1")
            apply_adjacency(nc, m, "a1", m.H, degrees=False)
            sum_neighbours(nc, m, "s1", m.H[:, :, :], m.AGGT)
            project_sum(nc, m)

            clear_semaphores(nc, m)
            normalise(nc, m, "n2")
        with ExitStack() as att:
            m.ALPHA = att.enter_context(nc.sbuf_tensor("ALPHA", [P, IB, HEADS, 32], F32))
            with ExitStack() as scoring:
                Q3 = scoring.enter_context(nc.sbuf_tensor("Q3", [P, NB, 3, FEAT], BF16))
                with ExitStack() as ph:
                    m.ps = psum(ph, "ps_qkv", [P, 8, 512])
                    project_qkv(nc, m, Q3)
                with ExitStack() as ph:
                    m.ps16 = psum(ph, "ps_hotT", [P, 2, 1024], BF16)
                    m.ps = psum(ph, "ps_terms", [P, 6, 512])
                    score_edges(nc, m, Q3)
            with ExitStack() as ph:
                m.ps = psum(ph, "ps_late", [P, 8, 512])
                softmax_edges(nc, m)
                m.ACC = att.enter_context(nc.sbuf_tensor("ACC", [P, 2, NB, FEAT + HEADS], F32))
                weigh_edges(nc, m)
                finish_attention(nc, m)
        with ExitStack() as ph:
            m.ps = psum(ph, "ps_end", [P, 8, 512])
            clear_semaphores(nc, m)
            normalise(nc, m, "n3", again=True)
            apply_adjacency(nc, m, "a3", m.D, degrees=False)
            sum_neighbours(nc, m, "s3", m.D[:, 0:NB, :], m.AGGT)
            project_pair(nc, m, "p3", m.W["W3a"], m.W["W3b"], m.brow["b3"], root=True)
            store_output(nc, m, out)



def lay_out(a):
    src, dst, attr = a["src"], a["dst"], a["edge_attr_32"]

    def tiled(v, pad, tiles):
        return np.concatenate([v, np.full(tiles * P - len(v), pad, v.dtype)]).reshape(tiles, P)

    edge = np.zeros(1, dst.dtype) - 1
    attr = np.concatenate([attr, np.zeros((TILES * P - EDGES, EDIM), attr.dtype)])
    w0, w3 = a["L0_gnn_W_out"].T, a["L3_gnn_W"].T
    out = {
        "x": a["x"],
        "src_rows": tiled(src, 0, KB * P), "dst_rows": tiled(dst, PAD_DST, KB * P),
        "prev_rows": tiled(np.concatenate([edge, dst[:-1]]), PAD_DST, KB * P),
        "next_rows": tiled(np.concatenate([dst[1:], edge]), PAD_DST, KB * P),
        "first_dst": dst[::P], "last_dst": np.concatenate([dst[P - 1::P], dst[-1:]])[:TILES],
        "src_pairs": tiled(src, 0, 2 * PKB * P).reshape(PKB * P, 2 * P),
        "dst_pairs": tiled(dst, PAD_DST, 2 * PKB * P).reshape(PKB * P, 2 * P),
        "first_dst2": dst[::2 * P], "last_dst2": np.concatenate([dst[2 * P - 1::2 * P], dst[-1:]])[:PAIRS],
        "src_cols": tiled(src, PAD_DST, TILES).T,
        "ea_tiles": attr.reshape(TILES, P, EDIM).transpose(0, 2, 1),
        "W0a": w0[:FEAT], "W0b": w0[FEAT:], "b0": a["L0_gnn_b_out"], "W1": a["L1_gnn_W"],
        "Wq": a["L2_gnn_Wq"], "bq": a["L2_gnn_bq"], "Wk": a["L2_gnn_Wk"], "bk": a["L2_gnn_bk"],
        "Wv": a["L2_gnn_Wv"], "bv": a["L2_gnn_bv"], "We": a["L2_gnn_We"],
        "Wskip": a["L2_gnn_Wskip"], "bskip": a["L2_gnn_bskip"],
        "M1": a["L2_gnn_W1"], "b1": a["L2_gnn_b1"], "M2": a["L2_gnn_W2"], "b2": a["L2_gnn_b2"],
        "gamma": a["L3_gnn_ln_gamma"], "beta": a["L3_gnn_ln_beta"],
        "W3a": w3[:FEAT], "W3b": w3[FEAT:], "b3": a["L3_gnn_b"],
    }
    return {n: np.ascontiguousarray(v) for n, v in out.items()}


def kernel(**inputs):
    import concourse.bacc as bacc
    from concourse.bass_utils import run_bass_kernel_spmd

    nc = bacc.Bacc("TRN2", target_bir_lowering=False, num_devices=1)
    arrays, tensors = {}, {}
    for name, a in lay_out({n: np.asarray(v) for n, v in inputs.items()}).items():
        arrays["in_" + name] = a
        tensors[name] = nc.dram_tensor("in_" + name, a.shape, mybir.dt.from_np(a.dtype), kind="ExternalInput").ap()
    out = nc.dram_tensor("out", [NODES, FEAT], F32, kind="ExternalOutput").ap()
    build(nc, tensors, out)
    return run_bass_kernel_spmd(nc, [arrays], core_ids=[0]).results[0]["out"]
```
